# Optimizing a Trainium2 kernel written in Bass

```python
import numpy as np
import jax
import jax.numpy as jnp

def _softmax(x, axis=-1):
    return jax.nn.softmax(x, axis=axis)

def _gelu(x):
    return jax.nn.gelu(x, approximate=True)

def _silu(x):
    return jax.nn.silu(x)

def _sigmoid(x):
    return jax.nn.sigmoid(x)

def _layernorm(x, axis=-1, eps=1e-05):
    m = jnp.mean(x, axis=axis, keepdims=True)
    v = jnp.var(x, axis=axis, keepdims=True)
    return (x - m) / jnp.sqrt(v + eps)

def _scatter_add(tgt, idx, src, axis=0):
    return tgt.at[idx].add(src)

def _segment_sum(src, seg, n):
    return jax.ops.segment_sum(src, seg, n)
kernel_name = 'mk_cond_resid_d4_seqx_r2_d2f28e'

def setup_inputs(seed: int=0):
    np.random.seed(seed)
    _w = jnp.asarray

    def _rec_inputs():
        import jax
        import jax.numpy as jnp
        _rk = jax.random.key(seed)
        x = -0.0001546 + 1 * jax.random.normal(jax.random.fold_in(_rk, 1), (8, 512, 512), jnp.float32)
        _lenS = 512 - jax.random.randint(jax.random.fold_in(_rk, 7), (8,), 0, max(1, 512 // 4) + 1, jnp.int32)
        _lenS2 = 512 - jax.random.randint(jax.random.fold_in(_rk, 8), (8,), 0, max(1, 512 // 4) + 1, jnp.int32)
        itok_B_1_98 = jax.random.randint(jax.random.fold_in(_rk, 11), (8,), 1, 99, jnp.int32)
        itok_B_0_7 = jax.random.randint(jax.random.fold_in(_rk, 12), (8,), 0, 8, jnp.int32)
        fside_BxSxS_0 = 4.13588e-05 + 0.999923 * jax.random.normal(jax.random.fold_in(_rk, 13), (8, 512, 512), jnp.float32)
        itok_B_18_1004 = jax.random.randint(jax.random.fold_in(_rk, 14), (8,), 18, 1005, jnp.int32)
        itok_B_0_30 = jax.random.randint(jax.random.fold_in(_rk, 15), (8,), 0, 31, jnp.int32)
        return (x, itok_B_1_98, itok_B_0_7, fside_BxSxS_0, itok_B_18_1004, itok_B_0_30)
    x, itok_B_1_98, itok_B_0_7, fside_BxSxS_0, itok_B_18_1004, itok_B_0_30 = _rec_inputs()

    def _L0_cond_setup():
        import jax, jax.numpy as jnp
        import numpy as np
        B = 128
        D = 512
        K = 100
        key = jax.random.key(seed)
        kx, kt, ks = jax.random.split(key, 3)
        x = jax.random.normal(kx, (B, D, D), dtype=jnp.float32)
        T = jax.random.normal(kt, (K, D, D), dtype=jnp.float32)
        fwd_steps = jax.random.randint(ks, (B,), 1, K + 1, dtype=jnp.int64)
        return {'x': x, 'fwd_steps': fwd_steps, 'T': T}
    _L0_cond_all = _L0_cond_setup()
    _L0_cond_in = {k: v for k, v in _L0_cond_all.items() if k in ('T',)}
    del _L0_cond_all

    def _L1_cond_setup():
        import jax, jax.numpy as jnp
        import numpy as np
        S, O, H = (8, 512, 512)
        B, N = (32, 256)
        key = jax.random.key(seed)
        k1, k2, k3, k4 = jax.random.split(key, 4)
        x = jax.random.normal(k1, (B, N, H), dtype=jnp.float32)
        subject_id = jax.random.randint(k2, (B,), 0, S)
        wbound = jnp.sqrt(2.0 / 6.0) * jnp.sqrt(3.0 / H)
        weight = jax.random.uniform(k3, (S, O, H), minval=-wbound, maxval=wbound, dtype=jnp.float32)
        bbound = 1.0 / jnp.sqrt(H)
        bias = jax.random.uniform(k4, (S, O), minval=-bbound, maxval=bbound, dtype=jnp.float32)
        return {'x': x, 'subject_id': subject_id, 'weight': weight, 'bias': bias}
    _L1_cond_all = _L1_cond_setup()
    _L1_cond_in = {k: v for k, v in _L1_cond_all.items() if k in ('weight', 'bias')}
    del _L1_cond_all

    def _L2_cond_setup():
        import jax, jax.numpy as jnp
        import numpy as np
        B, L1, L2, DIN, DOUT, H = (8, 512, 512, 512, 512, 16)
        DH = DOUT // H
        SCALE = 1.0 / np.sqrt(DH).astype(np.float32)
        key = jax.random.key(seed)
        ks = jax.random.split(key, 13)
        s = 0.02
        return {'seq1': jax.random.normal(ks[0], (B, L1, DIN), jnp.float32), 'seq2': jax.random.normal(ks[1], (B, L2, DIN), jnp.float32), 'seq_len1': jax.random.randint(ks[2], (B,), 1, L1 + 1, jnp.int32), 'Wq': jax.random.normal(ks[3], (DIN, DOUT), jnp.float32) * s, 'bq': jnp.zeros((DOUT,), jnp.float32), 'Wk': jax.random.normal(ks[4], (DIN, DOUT), jnp.float32) * s, 'bk': jnp.zeros((DOUT,), jnp.float32), 'Wv': jax.random.normal(ks[5], (DIN, DOUT), jnp.float32) * s, 'bv': jnp.zeros((DOUT,), jnp.float32), 'Wo': jax.random.normal(ks[6], (DOUT, DOUT), jnp.float32) * s, 'bo': jnp.zeros((DOUT,), jnp.float32), 'b_prev': jax.random.normal(ks[7], (1, 1, DIN), jnp.float32) * s, 'b_self': jax.random.normal(ks[8], (1, 1, DIN), jnp.float32) * s}
    _L2_cond_all = _L2_cond_setup()
    _L2_cond_in = {k: v for k, v in _L2_cond_all.items() if k in ('Wq', 'bq', 'Wk', 'bk', 'Wv', 'bv', 'Wo', 'bo', 'b_prev', 'b_self')}
    del _L2_cond_all

    def _L3_cond_setup():
        import jax, jax.numpy as jnp
        import numpy as np
        C, I, O = (32, 512, 512)
        B, T = (64, 256)
        key = jax.random.key(seed)
        kx, kc, kw, kb = jax.random.split(key, 4)
        x = jax.random.normal(kx, (B, T, I), dtype=jnp.float32)
        cat_ids = jax.random.randint(kc, (B,), 0, C)
        W = 0.02 * jax.random.normal(kw, (C, I, O), dtype=jnp.float32)
        b = jnp.zeros((C, O), dtype=jnp.float32)
        return {'x': x, 'cat_ids': cat_ids, 'W': W, 'b': b}
    _L3_cond_all = _L3_cond_setup()
    _L3_cond_in = {k: v for k, v in _L3_cond_all.items() if k in ('W', 'b')}
    del _L3_cond_all
    return {'x': x, 'itok_B_1_98': itok_B_1_98, 'itok_B_0_7': itok_B_0_7, 'fside_BxSxS_0': fside_BxSxS_0, 'itok_B_18_1004': itok_B_18_1004, 'itok_B_0_30': itok_B_0_30, 'L0_cond_T': _L0_cond_in['T'], 'L1_cond_weight': _L1_cond_in['weight'], 'L1_cond_bias': _L1_cond_in['bias'], 'L2_cond_Wq': _L2_cond_in['Wq'], 'L2_cond_bq': _L2_cond_in['bq'], 'L2_cond_Wk': _L2_cond_in['Wk'], 'L2_cond_bk': _L2_cond_in['bk'], 'L2_cond_Wv': _L2_cond_in['Wv'], 'L2_cond_bv': _L2_cond_in['bv'], 'L2_cond_Wo': _L2_cond_in['Wo'], 'L2_cond_bo': _L2_cond_in['bo'], 'L2_cond_b_prev': _L2_cond_in['b_prev'], 'L2_cond_b_self': _L2_cond_in['b_self'], 'L3_cond_W': _L3_cond_in['W'], 'L3_cond_b': _L3_cond_in['b']}

def reference(x, itok_B_1_98, itok_B_0_7, fside_BxSxS_0, itok_B_18_1004, itok_B_0_30, L0_cond_T, L1_cond_weight, L1_cond_bias, L2_cond_Wq, L2_cond_bq, L2_cond_Wk, L2_cond_bk, L2_cond_Wv, L2_cond_bv, L2_cond_Wo, L2_cond_bo, L2_cond_b_prev, L2_cond_b_self, L3_cond_W, L3_cond_b):
    import jax
    import jax.numpy as jnp

    def _L0_cond_ref(x, fwd_steps, T):
        import jax, jax.numpy as jnp
        import numpy as np
        B = 128
        D = 512
        K = 100
        Tb = T[fwd_steps - 1]
        return jnp.einsum('bij,bjk->bik', Tb, x)

    def _L1_cond_ref(x, subject_id, weight, bias):
        import jax, jax.numpy as jnp
        import numpy as np
        S, O, H = (8, 512, 512)
        B, N = (32, 256)
        W = weight[subject_id]
        b = bias[subject_id]
        y = jnp.einsum('bnh,boh->bno', x, W) + b[:, None, :]
        return y

    def _L2_cond_ref(seq1, seq2, seq_len1, Wq, bq, Wk, bk, Wv, bv, Wo, bo, b_prev, b_self):
        import jax, jax.numpy as jnp
        import numpy as np
        B, L1, L2, DIN, DOUT, H = (8, 512, 512, 512, 512, 16)
        DH = DOUT // H
        SCALE = 1.0 / np.sqrt(DH).astype(np.float32)
        b, l1, _ = seq1.shape
        l2 = seq2.shape[1]
        query = seq2 + b_self
        key = jnp.concatenate([seq1 + b_prev, seq2 + b_self], 1)
        value = jnp.concatenate([seq1, seq2], 1)
        q = (query @ Wq + bq).reshape(b, l2, H, DH).transpose(0, 2, 1, 3)
        k = (key @ Wk + bk).reshape(b, l1 + l2, H, DH).transpose(0, 2, 1, 3)
        v = (value @ Wv + bv).reshape(b, l1 + l2, H, DH).transpose(0, 2, 1, 3)
        score_prev = jnp.einsum('bhqd,bhkd->bhqk', q, k[:, :, :l1]) * SCALE
        score_self = (q * k[:, :, l1:]).sum(-1, keepdims=True) * SCALE
        mask = jnp.arange(l1)[None, :] < seq_len1[:, None]
        score_prev = jnp.where(mask[:, None, None, :], score_prev, -jnp.inf)
        score = jnp.concatenate([score_prev, score_self], -1)
        weights = jax.nn.softmax(score, axis=-1)
        attn = jnp.einsum('bhqk,bhkd->bhqd', weights[..., :-1], v[:, :, :l1])
        attn = attn + weights[..., -1:] * v[:, :, l1:]
        attn = attn.transpose(0, 2, 1, 3).reshape(b, l2, H * DH)
        return attn @ Wo + bo

    def _L3_cond_ref(x, cat_ids, W, b):
        import jax, jax.numpy as jnp
        import numpy as np
        C, I, O = (32, 512, 512)
        B, T = (64, 256)
        selected_W = W[cat_ids]
        selected_b = b[cat_ids]
        if x.ndim == 2:
            return jnp.einsum('bi,bio->bo', x, selected_W) + selected_b
        return jnp.einsum('bti,bio->bto', x, selected_W) + selected_b[:, None, :]
    x = x + _L0_cond_ref(x, itok_B_1_98, L0_cond_T)
    x = x + _L1_cond_ref(x, itok_B_0_7, L1_cond_weight, L1_cond_bias)
    x = x + _L2_cond_ref(x, fside_BxSxS_0, itok_B_18_1004, L2_cond_Wq, L2_cond_bq, L2_cond_Wk, L2_cond_bk, L2_cond_Wv, L2_cond_bv, L2_cond_Wo, L2_cond_bo, L2_cond_b_prev, L2_cond_b_self)
    x = x + _L3_cond_ref(x, itok_B_0_30, L3_cond_W, L3_cond_b)
    return x

_drawn_inputs = setup_inputs


def setup_inputs(seed=0):
    import zlib

    import numpy as np

    out = dict(_drawn_inputs(seed))
    spreads = {'L2_cond_bq': (0.0, 0.1),
     'L2_cond_bk': (0.0, 2.0),
     'L2_cond_bv': (0.0, 2.0),
     'L2_cond_bo': (0.0, 2.0),
     'L3_cond_b': (0.0, 2.0)}
    factors = {'L1_cond_bias': 59.167, 'L2_cond_b_prev': 64.0, 'L2_cond_b_self': 8.0}
    for name, (base, spread) in spreads.items():
        noise = np.random.default_rng([zlib.crc32(name.encode()), seed]).standard_normal(out[name].shape)
        drawn = base * np.exp(spread * noise) if base else spread * noise
        out[name] = jnp.asarray(drawn.astype(out[name].dtype))
    for name, factor in factors.items():
        out[name] = (out[name] * factor).astype(out[name].dtype)
    return out
```

```python
from contextlib import ExitStack

import concourse.bass as bass
from concourse import mybir

F32 = mybir.dt.float32
F32R = mybir.dt.float32r
I32 = mybir.dt.int32
ALU = mybir.AluOpType
ACT = mybir.ActivationFunctionType
AX = mybir.AxisListType

P = 128
B = 8
D = 512
C = D // P
DH = 32
G = 4
HG = P // DH
SCALE = float(DH) ** -0.5
MASKED = -1e30
ROW_MASK = 3 * DH
ROW_MAX = 3 * DH + 1
K_MAX = 3 * DH + 1
K_ALL = 3 * DH + 2

RAW_SETUP = 4
RAW_L0 = 3
RAW_BODY = 6
UNITS_L0 = C
UNITS_BODY = 9 * C
U_L1, U_PROJ0, U_V, U_PROJ, U_L0 = 0, C, 2 * C, 3 * C, 6 * C
UNIT_Q, UNIT_KSELF, UNIT_VSELF, UNIT_K = range(4)
TILES = 2 * C


def build(nc, x_blk, xT, Tt, w1_blk, b1, seqT, wq, wk, wv, wo, bq, bk, bv, bo, b_prev, b_self,
          w3_blk, b3, steps, subjects, lengths, cats, consts, iota, out):
    with ExitStack() as ctx:
        def sb(name, shape, dt=F32):
            return ctx.enter_context(nc.sbuf_tensor(name, shape, dt))

        def sem(name):
            return ctx.enter_context(nc.semaphore(name))

        wq_s = sb("wq_s", [P, 2, C, D], F32R)
        wk_s = sb("wk_s", [P, 2, C, D], F32R)
        wv_s = sb("wv_s", [P, 2, C, D], F32R)
        wo_s = sb("wo_s", [P, 2, C, D], F32R)
        kst = sb("kst", [P, 2, HG, D], F32R)
        qst = sb("qst", [P, 2, HG, D], F32R)
        x1h, x1l = kst[:, 0], qst[:, 0]
        ts_s = sb("ts_s", [P, 2, C, D], F32R)
        x2_s = sb("x2_s", [P, 2, C, D], F32R)
        at_s = sb("at_s", [P, 2, C, D], F32R)
        xres = sb("xres", [P, C, D])
        wblk = sb("wblk", [P, 2, 2, D], F32R)
        raw = sb("raw", [P, C, D])
        v_sb = sb("v_sb", [P, C, D])
        probs = sb("probs", [P, 2, 2, D])
        q_f = sb("q_f", [P, D])
        q_hi = sb("q_hi", [P, D], F32R)
        q_lo = sb("q_lo", [P, D], F32R)
        k_hi = sb("k_hi", [P, D], F32R)
        k_lo = sb("k_lo", [P, D], F32R)
        mx_rep = k_lo[:, :].bitcast(F32)
        vself = sb("vself", [P, 2, D])
        nself = sb("nself", [P, D])
        negm = sb("negm", [P, D], F32R)
        num = sb("num", [P, D])
        den = sb("den", [P, D])
        mx = sb("mx", [P, C, HG])
        cst = sb("cst", [P, 2 * P + DH])
        ident, blocks, ones = cst[:, 0:P], cst[:, P:2 * P], cst[:, 2 * P:]
        bcol = sb("bcol", [P, 7, C])
        BQ, BKSELF, BK, BV, BO, B1, B3 = range(7)
        bvec = sb("bvec", [P, 2, C])
        bvs = sb("bvs", [P, 2, C, 2], F32R)
        idx = sb("idx", [1, 3, B], I32)
        len_i = sb("len_i", [B, 1], I32)
        len_f = sb("len_f", [B, 1])
        masks = nc.dram_tensor("masks", (B + 1, D), F32, kind="Internal").ap()

        gb = [ctx.enter_context(nc.psum_tensor(f"gb{n}", [P, D], F32)) for n in range(2)]
        sc = [ctx.enter_context(nc.psum_tensor(f"sc{n}", [P, 2, D], F32)) for n in range(2)]
        pv = ctx.enter_context(nc.psum_tensor("pv", [P, D], F32))
        dn = ctx.enter_context(nc.psum_tensor("dn", [P, D], F32))

        consts_in, mask_made, mask_kept = sem("consts_in"), sem("mask_made"), sem("mask_kept")
        w_hi, w_lo = sem("w_hi"), sem("w_lo")
        bias_mm, bias_ready = sem("bias_mm"), sem("bias_ready")
        raw_in = [sem(f"raw_in{s}") for s in range(C)]
        w1_hi, w1_lo = sem("w1_hi"), sem("w1_lo")
        xb_hi, xb_lo = sem("xb_hi"), sem("xb_lo")
        w3_hi, w3_lo = sem("w3_hi"), sem("w3_lo")
        t_hi, t_lo = sem("t_hi"), sem("t_lo")
        sq_hi, sq_lo = sem("sq_hi"), sem("sq_lo")
        gemm_ready = sem("gemm_ready")
        x1_sum, x1_hi, x1_lo = sem("x1_sum"), sem("x1_hi"), sem("x1_lo")
        x2_part, x2_sum, x2_hi, x2_lo = sem("x2_part"), sem("x2_sum"), sem("x2_hi"), sem("x2_lo")
        x3_sum, x3_hi, x3_lo = sem("x3_sum"), sem("x3_hi"), sem("x3_lo")
        out_ready, out_kept = sem("out_ready"), sem("out_kept")
        b1_in, b3_in = sem("b1_in"), sem("b3_in")
        q_ready, qhi_ready, q_split = sem("q_ready"), sem("qhi_ready"), sem("q_split")
        prod_ready, vself_ready, v_ready = sem("prod_ready"), sem("vself_ready"), sem("v_ready")
        khi_ready, k_split = sem("khi_ready"), sem("k_split")
        qst_in = [sem(f"qst_in{s}") for s in range(2)]
        kst_in = [sem(f"kst_in{s}") for s in range(2)]
        s_ready, red_ready = sem("s_ready"), sem("red_ready")
        mxrep_ready, mt_ready = sem("mxrep_ready"), sem("mt_ready")
        ss_ready, nself_ready = sem("ss_ready"), sem("nself_ready")
        negm_ready, negm_in = sem("negm_ready"), sem("negm_in")
        arg_ready, eself_ready, wself_ready = sem("arg_ready"), sem("eself_ready"), sem("wself_ready")
        probs_ready, probs_used = sem("probs_ready"), sem("probs_used")
        den_ready, fin_read = sem("den_ready"), sem("fin_read")
        recip_ready, norm_ready, at_hi, at_lo = sem("recip_ready"), sem("norm_ready"), sem("at_hi"), sem("at_lo")

        def wait(eng, s, value):
            if not (isinstance(value, int) and value <= 0):
                eng.wait_ge(s, value)

        def units(i):
            return UNITS_L0 + UNITS_BODY * i

        def raws(i):
            return RAW_SETUP + RAW_L0 + RAW_BODY * i

        def raw_shared(w, n):
            return n, w + 1

        def raw_l0(i, n):
            return n % C, (RAW_SETUP if isinstance(i, int) and i == 0 else raws(i - 1) + 2) + n // C + 1

        def raw_w1(i, m):
            return m, raws(i) + 1

        def raw_seq(i, kc):
            return kc, raws(i) + 2

        def raw_w3(i, m, last):
            return m, raws(i) + (3 if last else RAW_BODY)

        def q_filled(i, g):
            return 16 * ((2 * i + g // 2 + 1) * 3 * HG + i + 1)

        def k_filled(i, g):
            return 16 * ((2 * i + g // 2 + 1) * 3 * HG + 2 * (i + 1))

        def cols(m):
            return slice(P * m, P * m + P)

        block = ctx.enter_context(nc.Block())

        @block.sync
        def _(sp):
            def flat(src):
                return src.rearrange("a p n -> (a p) n")

            def load(src, slot_count, used, value):
                slot, _ = slot_count
                wait(sp, used, value)
                sp.dma_start(raw[:, slot], src).then_inc(raw_in[slot], 16)

            for dst, src in ((cst[:, :], consts), (bvec[:, 0, :], b_self), (bvec[:, 1, :], b_prev),
                             (bcol[:, BQ], bq), (bcol[:, BKSELF], bk), (bcol[:, BK], bk),
                             (bcol[:, BV], bv), (bcol[:, BO], bo),
                             (idx[0:1, 0, :], steps), (idx[0:1, 1, :], subjects), (idx[0:1, 2, :], cats),
                             (len_i[:, :], lengths), (xres[0:B, 0, :], iota)):
                sp.dma_start(dst, src).then_inc(consts_in, 16)

            def index(which, i, least, most):
                return sp.value_load(idx[0:1, which, bass.ds(i, 1)], min_val=least, max_val=most)

            def load_t(i, used, value):
                t = index(0, i, 1, 100) - 1
                for n in range(C):
                    load(flat(Tt[bass.ds(t, 1), n]), raw_l0(i, n), used, value + n + 1)

            def load_x(i):
                for n in range(C, 3 * C):
                    m = (n - C) // 2
                    src = flat((x_blk if n % 2 == 0 else xT)[bass.ds(i, 1), m])
                    if n < 2 * C:
                        load(src, raw_l0(i, n), t_lo, C * i + n - C + 1)
                    else:
                        load(src, raw_l0(i, n), (xb_lo, x1_lo)[n % 2], C * i + m - 2 + 1)

            def load_w1(i):
                s = index(1, i, 0, 7)
                wait(sp, x2_part, C * i)
                sp.dma_start(bcol[:, B1], flat(b1[bass.ds(s, 1)])).then_inc(b1_in, 16)
                for m in range(C):
                    if isinstance(i, int) and i == 0:
                        load(flat(w1_blk[bass.ds(s, 1), m]), raw_w1(i, m), (xb_lo, x1_lo)[m % 2], 2 + m // 2 + 1)
                    else:
                        load(flat(w1_blk[bass.ds(s, 1), m]), raw_w1(i, m), w3_lo, C * (i - 1) + m + 1)

            def fill(stack, s, parts, filled):
                for n, part in enumerate(parts):
                    for h in range(HG):
                        sp.dma_start(stack[DH * n:DH * n + DH, s, h].bitcast(F32),
                                     part[DH * h:DH * h + DH, :].bitcast(F32)).then_inc(filled, 16)

            def fill_row(stack, row, s, source, filled):
                sp.dma_start(stack[row:row + 1, s].bitcast(F32),
                             source.rearrange("a (o n) -> a o n", o=1).to_broadcast([1, HG, D])).then_inc(filled, 16)

            def fill_q(i, g):
                s = g % 2
                sp.wait_ge(q_split, G * i + g + 1)
                fill(qst, s, (q_hi, q_lo, q_hi), qst_in[s])
                if g < 2:
                    fill_row(qst, ROW_MASK, s, masks[B:B + 1, :], qst_in[s])

            def fill_k(i, g):
                s = g % 2
                sp.wait_ge(k_split, G * i + g + 1)
                fill(kst, s, (k_hi, k_hi, k_lo), kst_in[s])
                if g < 2:
                    fill_row(kst, ROW_MASK, s, masks[bass.ds(i, 1), :], kst_in[s])
                    fill_row(kst, ROW_MAX, s, masks[B:B + 1, :], kst_in[s])

            def fill_max(i, g):
                sp.wait_ge(negm_ready, G * i + g + 1)
                sp.dma_start(qst[ROW_MAX:ROW_MAX + 1, g % 2].bitcast(F32), negm[0:P:DH, :].bitcast(F32)
                             ).then_inc(negm_in, 16)

            def body(i, last):
                for kc in range(C):
                    load(flat(seqT[bass.ds(i, 1), kc]), raw_seq(i, kc), w1_lo, C * i + kc + 1)
                fill_q(i, 0)
                fill_k(i, 0)
                if not last:
                    load_t(i + 1, sq_lo, C * i)
                for g in range(G):
                    if g < G - 1:
                        fill_q(i, g + 1)
                    elif not last:
                        load_x(i + 1)
                    fill_max(i, g)
                    if g < G - 1:
                        fill_k(i, g + 1)
                c = index(2, i, 0, 31)
                wait(sp, out_ready, C * i)
                sp.dma_start(bcol[:, B3], flat(b3[bass.ds(c, 1)])).then_inc(b3_in, 16)
                for m in range(C):
                    used, value = ((sq_lo, C * i + m + 1) if last
                                   else ((xb_lo, x1_lo)[m % 2], C * (i + 1) + 2 + m // 2 + 1))
                    load(flat(w3_blk[bass.ds(c, 1), m]), raw_w3(i, m, last), used, value)
                if not last:
                    load_w1(i + 1)
                for m in range(C):
                    sp.wait_ge(out_ready, C * i + m + 1)
                    sp.dma_start(flat(out[bass.ds(i, 1), m]), xres[:, m]).then_inc(out_kept, 16)

            for w, src in enumerate((wq, wk, wv, wo)):
                for n in range(C):
                    load(src[n], raw_shared(w, n), w_lo, 1 + C * (w - 1) + n + 1 if w else 0)
            sp.wait_ge(consts_in, 13 * 16)
            load_t(0, w_lo, 1 + 3 * C)
            sp.wait_ge(mask_made, 3)
            sp.dma_start(masks[0:B, :], xres[0:B, 1, :]).then_inc(mask_kept, 16)
            sp.dma_start(masks[B:B + 1, :], xres[0:1, 2, :]).then_inc(mask_kept, 16)
            load_x(0)
            load_w1(0)
            sp.wait_ge(mask_kept, 32)
            body(0, False)
            with sp.Fori(1, B - 1) as i:
                body(i, False)
            body(B - 1, True)
            sp.wait_ge(out_kept, 16 * C * B)

        @block.tensor
        def _(pe):
            def product(dst, lhs, rhs, start, stop):
                pe.matmul(dst, lhs(0), rhs(0), start=start, stop=False)
                pe.matmul(dst, lhs(0), rhs(1), start=False, stop=False)
                return pe.matmul(dst, lhs(1), rhs(0), start=False, stop=stop)

            def chunk(m, kc, lhs, rhs, emptied):
                if kc == 0:
                    wait(pe, *emptied)
                last = product(gb[m % 2][:, :], lhs, rhs, kc == 0, kc == C - 1)
                if kc == C - 1:
                    last.then_inc(gemm_ready, 1)

            def l0(i, m, kc, before):
                if kc == 0:
                    pe.wait_ge(xb_lo, C * i + m + 1)
                if m == 0:
                    pe.wait_ge(t_lo, C * i + kc + 1)
                chunk(m, kc, lambda h: wblk[:, m % 2, h, cols(kc)], lambda h: ts_s[:, h, kc],
                      before[m] if m < 2 else (x1_sum, C * i + m - 1))

            def l1(i, m, kc):
                if kc == 0:
                    pe.wait_ge(w1_lo, C * i + m + 1)
                if m == 0:
                    pe.wait_ge(x1_lo, C * i + kc + 1)
                first = isinstance(i, int) and i == 0
                chunk(m, kc, lambda h: wblk[:, m % 2, h, cols(kc)], lambda h: (x1h, x1l)[h][:, kc],
                      (x2_part, C * i + m - 1) if m >= 2 else
                      (x1_sum, m + 3) if first else (out_ready, C * (i - 1) + m + 3))

            def projection(i, g, m, kc):
                if g == 0 and m == UNIT_Q:
                    pe.wait_ge(sq_lo, C * i + kc + 1)
                if g == 0 and m == UNIT_K:
                    pe.wait_ge(x2_lo, C * i + kc + 1)
                w = (wq_s, wk_s, wv_s, wk_s)[m]
                rhs = x2_s if m == UNIT_K else ts_s
                if m < 2:
                    emptied = ((x2_part, C * i + m + 3) if g == 0 else (v_ready, C * i + m + 3) if g == 1
                               else ((vself_ready, k_split)[m], G * i + g))
                else:
                    emptied = (q_ready, prod_ready)[m % 2], G * i + g + 1
                chunk(m, kc, lambda h: w[:, h, kc, cols(g)], lambda h: rhs[:, h, kc], emptied)

            def values(i, m, kc):
                chunk(m, kc, lambda h: x2_s[:, h, kc, cols(m)], lambda h: wv_s[:, h, kc],
                      (v_ready, C * i + m - 1) if m >= 2 else ((vself_ready, k_split)[m], G * i + 1))

            def l2_out(i, last, m, kc):
                if m == 0:
                    pe.wait_ge(at_lo, G * i + kc + 1)
                chunk(m, kc, lambda h: wo_s[:, h, kc, cols(m)], lambda h: at_s[:, h, kc],
                      (x3_sum, C * i + m - 1) if m >= 2 else
                      ((vself_ready, k_split)[m], G * i + G) if last else (x1_sum, C * (i + 1) + m + 3))

            def l3(i, m, kc):
                if kc == 0:
                    pe.wait_ge(w3_lo, C * i + m + 1)
                if m == 0:
                    pe.wait_ge(x3_lo, C * i + kc + 1)
                chunk(m, kc, lambda h: wblk[:, m % 2, h, cols(kc)], lambda h: x2_s[:, h, kc],
                      (out_ready, C * i + m - 1) if m >= 2 else (x3_sum, C * i + m + 3))

            def in_turns(step):
                for m, kc in [(m, kc) for m in (0, 1) for kc in range(C - 1)] + [(0, C - 1), (1, C - 1)]:
                    step(m, kc)
                for m in range(2, C):
                    for kc in range(C):
                        step(m, kc)

            def score_tile(t, lhs, rhs):
                for j in range(2):
                    mm = pe.matmul(sc[t % 2][:, j], lhs(j), rhs(j), start=True, stop=True)
                mm.then_inc(s_ready, 1)

            def body(i, last):
                for m in range(C):
                    for kc in range(C):
                        l1(i, m, kc)
                for m in range(C):
                    for kc in range(C):
                        projection(i, 0, m, kc)
                for m in range(C):
                    for kc in range(C):
                        values(i, m, kc)

                for g in range(G):
                    slot, group = g % 2, G * i + g
                    before_l0 = ((vself_ready, G * i + G), (k_split, G * i + G))

                    def beside(n):
                        if g < G - 1:
                            projection(i, g + 1, n // C, n % C)
                        elif not last:
                            l0(i + 1, n // C, n % C, before_l0)

                    pe.wait_ge(qst_in[slot], q_filled(i, g))
                    pe.wait_ge(kst_in[slot], k_filled(i, g))
                    for t in range(TILES):
                        c, h0 = t // 2, 2 * (t % 2)
                        if t < 2:
                            wait(pe, probs_ready, TILES * group - 1 + t)
                        else:
                            pe.wait_ge(red_ready, TILES * group + t - 1)
                        score_tile(t, lambda j: qst[0:K_MAX, slot, h0 + j, cols(c)],
                                   lambda j: kst[0:K_MAX, slot, h0 + j, :])
                        beside(t)
                        if t == C - 1:
                            pe.wait_ge(prod_ready, group + 1)
                            wait(pe, fin_read, group)
                            pe.matmul(dn[:, :], blocks, q_f[:, :], start=True, stop=True).then_inc(ss_ready, 1)
                    for n in range(8, 11):
                        beside(n)
                    pe.wait_ge(mxrep_ready, group + 1)
                    for c in range(C):
                        mm = pe.transpose(pv[:, cols(c)], mx_rep[:, cols(c)], ident)
                    mm.then_inc(mt_ready, 1)
                    for n in range(11, 16):
                        beside(n)

                    def prob_scores(t):
                        c, h0 = t // 2, 2 * (t % 2)
                        score_tile(t, lambda j: kst[0:K_ALL, slot, h0 + j, cols(c)],
                                   lambda j: qst[0:K_ALL, slot, h0 + j, :])

                    pe.wait_ge(negm_in, 16 * (group + 1))
                    pe.wait_ge(nself_ready, group + 1)
                    if g == 0:
                        pe.wait_ge(v_ready, C * i + C)
                    for t in range(2):
                        pe.wait_ge(red_ready, TILES * group + TILES - 1 + t)
                        prob_scores(t)
                    for t in range(TILES):
                        c, h0 = t // 2, 2 * (t % 2)
                        pe.wait_ge(probs_ready, TILES * group + t + 1)
                        for j in range(2):
                            h = h0 + j
                            rows = slice(DH * h, DH * h + DH)
                            feats = slice(P * g + DH * h, P * g + DH * h + DH)
                            pe.matmul(pv[rows, :], v_sb[:, c, feats], probs[:, t % 2, j], start=(c == 0),
                                      stop=(c == C - 1), tile_position=(0, DH * h))
                            mm = pe.matmul(dn[rows, :], ones, probs[:, t % 2, j], start=(c == 0),
                                           stop=(c == C - 1), tile_position=(0, DH * h))
                        mm.then_inc(probs_used, 1)
                        if t + 2 < TILES:
                            prob_scores(t + 2)

                in_turns(lambda m, kc: l2_out(i, last, m, kc))
                in_turns(lambda m, kc: l3(i, m, kc))

            pe.wait_ge(w_lo, 1 + 2 * C)
            for n, w in enumerate((wq_s, wk_s)):
                for m in range(C):
                    for kc in range(C):
                        mm = product(gb[n][:, 2 * m:2 * m + 2], lambda h: w[:, h, kc, cols(m)],
                                     lambda h: bvs[:, h, kc], kc == 0, kc == C - 1)
                mm.then_inc(bias_mm, 1)
            for m in range(C):
                for kc in range(C):
                    l0(0, m, kc, ((bias_ready, 1), (bias_ready, 3)))
            pe.wait_ge(w_lo, 1 + 4 * C)
            pe.wait_ge(consts_in, 13 * 16)
            body(0, False)
            with pe.Fori(1, B - 1) as i:
                body(i, False)
            body(B - 1, True)

        @block.scalar
        def _(act):
            def hi(dst, slot_count, ready):
                slot, count = slot_count
                act.wait_ge(raw_in[slot], 16 * count)
                act.activation(dst, raw[:, slot], ACT.Copy).then_inc(ready, 1)

            def project_q(i, g, first):
                act.wait_ge(gemm_ready, units(i) + first + UNIT_Q + 1)
                act.activation(q_f[:, :], gb[UNIT_Q % 2][:, :], ACT.Identity, bias=bcol[:, BQ, g:g + 1]
                               ).then_inc(q_ready, 1)

            def project_vk(i, g, first):
                act.wait_ge(gemm_ready, units(i) + first + UNIT_VSELF + 1)
                act.activation(vself[:, g % 2], gb[UNIT_VSELF % 2][:, :], ACT.Copy).then_inc(vself_ready, 1)
                act.wait_ge(gemm_ready, units(i) + first + UNIT_K + 1)
                act.activation(k_hi[:, :], gb[UNIT_K % 2][:, :], ACT.Identity, bias=bcol[:, BK, g:g + 1]
                               ).then_inc(khi_ready, 1)

            def body(i, last):
                for m in range(2):
                    act.wait_ge(gemm_ready, units(i) - 2 + m + 1)
                    hi(wblk[:, m % 2, 0], raw_w1(i, m), w1_hi)
                for kc in range(2):
                    hi(ts_s[:, 0, kc], raw_seq(i, kc), sq_hi)
                for m in range(2, C):
                    act.wait_ge(gemm_ready, units(i) + U_L1 + m - 1)
                    hi(wblk[:, m % 2, 0], raw_w1(i, m), w1_hi)
                for kc in range(2, C):
                    hi(ts_s[:, 0, kc], raw_seq(i, kc), sq_hi)
                project_q(i, 0, U_PROJ0)
                project_vk(i, 0, U_PROJ0)
                for m in range(C):
                    act.wait_ge(gemm_ready, units(i) + U_V + m + 1)
                    act.activation(v_sb[:, m], gb[m % 2][:, :], ACT.Copy).then_inc(v_ready, 1)

                for g in range(G):
                    group, first = G * i + g, U_PROJ + C * g
                    act.wait_ge(ss_ready, group + 1)
                    act.activation(nself[:, :], dn[:, :], ACT.Copy, scale=-1.0).then_inc(nself_ready, 1)
                    if g < G - 1:
                        project_q(i, g + 1, first)
                        project_vk(i, g + 1, first)
                    if g == G - 2 and not last:
                        for kc in range(C):
                            hi(ts_s[:, 0, kc], raw_l0(i + 1, kc), t_hi)
                        for m in range(2):
                            hi(wblk[:, m % 2, 0], raw_l0(i + 1, C + 2 * m), xb_hi)
                    if g == G - 1 and not last:
                        for m in range(2, C):
                            act.wait_ge(gemm_ready, units(i) + U_L0 + m - 1)
                            hi(wblk[:, m % 2, 0], raw_l0(i + 1, C + 2 * m), xb_hi)
                    for t in range(TILES):
                        act.wait_ge(s_ready, 2 * TILES * group + TILES + t + 1)
                        wait(act, probs_used, TILES * group + t - 1)
                        act.activation(probs[:, t % 2], sc[t % 2][:, :, :], ACT.Exp, scale=SCALE
                                       ).then_inc(probs_ready, 1)
                        if t == 1:
                            act.wait_ge(arg_ready, group + 1)
                            act.activation(nself[:, :], nself[:, :], ACT.Exp, scale=SCALE).then_inc(eself_ready, 1)
                for m in range(C):
                    act.wait_ge(gemm_ready, units(i) + (
                        (U_L1 + m + 3 if last else U_L0 + m + 3) if m < 2
                        else U_L0 + (C if last else 2 * C) + m - 1))
                    hi(wblk[:, m % 2, 0], raw_w3(i, m, last), w3_hi)

            act.wait_ge(consts_in, 13 * 16)
            act.activation(bvs[:, 0], bvec[:, :, :].rearrange("p v c -> p c v"), ACT.Copy).then_inc(w_hi, 1)
            for w, dst in enumerate((wq_s, wk_s, wv_s, wo_s)):
                for kc in range(C):
                    hi(dst[:, 0, kc], raw_shared(w, kc), w_hi)
            for kc in range(C):
                hi(ts_s[:, 0, kc], raw_l0(0, kc), t_hi)
            for m in range(C):
                if m >= 2:
                    act.wait_ge(gemm_ready, m - 1)
                hi(wblk[:, m % 2, 0], raw_l0(0, C + 2 * m), xb_hi)
            body(0, False)
            with act.Fori(1, B - 1) as i:
                body(i, False)
            body(B - 1, True)

        @block.gpsimd
        def _(pool):
            def lo(dst, hi_part, slot, hi_ready, count, ready):
                pool.wait_ge(hi_ready, count)
                pool.tensor_tensor(dst, raw[:, slot], hi_part.bitcast(F32), ALU.subtract).then_inc(ready, 1)

            def body(i, last):
                for m in range(2):
                    lo(wblk[:, m % 2, 1], wblk[:, m % 2, 0], m, w1_hi, C * i + m + 1, w1_lo)
                for kc in range(2):
                    lo(ts_s[:, 1, kc], ts_s[:, 0, kc], kc, sq_hi, C * i + kc + 1, sq_lo)
                for m in range(2, C):
                    lo(wblk[:, m % 2, 1], wblk[:, m % 2, 0], m, w1_hi, C * i + m + 1, w1_lo)
                for kc in range(2, C):
                    lo(ts_s[:, 1, kc], ts_s[:, 0, kc], kc, sq_hi, C * i + kc + 1, sq_lo)
                for g in range(G):
                    group = G * i + g
                    pool.wait_ge(negm_ready, group + 1)
                    pool.tensor_tensor(nself[:, :], negm[:, :].bitcast(F32), nself[:, :], ALU.subtract
                                       ).then_inc(arg_ready, 1)
                    pool.wait_ge(eself_ready, group + 1)
                    pool.tensor_tensor(vself[:, g % 2], vself[:, g % 2], nself[:, :], ALU.mult
                                       ).then_inc(wself_ready, 1)
                for m in range(C):
                    lo(wblk[:, m % 2, 1], wblk[:, m % 2, 0], m, w3_hi, C * i + m + 1, w3_lo)

            body(0, False)
            with pool.Fori(1, B - 1) as i:
                body(i, False)
            body(B - 1, True)

        @block.vector
        def _(dve):
            def lo(dst, hi_part, slot, hi_ready, count, ready):
                dve.wait_ge(hi_ready, count)
                dve.tensor_tensor(dst, raw[:, slot], hi_part.bitcast(F32), ALU.subtract).then_inc(ready, 1)

            def split(src, hi_part, lo_part, summed, hi_ready, lo_ready, count):
                dve.wait_ge(summed, count)
                dve.tensor_copy(hi_part, src).then_inc(hi_ready, 1)
                dve.wait_ge(hi_ready, count)
                dve.tensor_tensor(lo_part, src, hi_part.bitcast(F32), ALU.subtract).then_inc(lo_ready, 1)

            def t_lo_block(i, kc):
                lo(ts_s[:, 1, kc], ts_s[:, 0, kc], kc, t_hi, C * i + kc + 1, t_lo)

            def x_lo_block(i, m):
                lo(wblk[:, m % 2, 1], wblk[:, m % 2, 0], (2 * m) % C, xb_hi, C * i + m + 1, xb_lo)

            def sum_x1(i, m, unit):
                slot, count = raw_l0(i, C + 2 * m + 1)
                dve.wait_ge(raw_in[slot], 16 * count)
                dve.wait_ge(gemm_ready, unit + m + 1)
                dve.tensor_tensor(raw[:, slot], gb[m % 2][:, :], raw[:, slot], ALU.add).then_inc(x1_sum, 1)
                split(raw[:, slot], x1h[:, m], x1l[:, m], x1_sum, x1_hi, x1_lo, C * i + m + 1)

            def sum_x2(i, m):
                dve.wait_ge(gemm_ready, units(i) + U_L1 + m + 1)
                dve.scalar_tensor_tensor(out=xres[:, m], in0=gb[m % 2][:, :], scalar=bcol[:, B1, m:m + 1],
                                         in1=x1h[:, m].bitcast(F32), op0=ALU.add, op1=ALU.add).then_inc(x2_part, 1)
                dve.wait_ge(x2_part, C * i + m + 1)
                dve.tensor_tensor(xres[:, m], xres[:, m], x1l[:, m].bitcast(F32), ALU.add).then_inc(x2_sum, 1)
                split(xres[:, m], x2_s[:, 0, m], x2_s[:, 1, m], x2_sum, x2_hi, x2_lo, C * i + m + 1)

            def add_to_xres(unit, m, bias, ready):
                dve.wait_ge(gemm_ready, unit + m + 1)
                dve.scalar_tensor_tensor(out=xres[:, m], in0=gb[m % 2][:, :], scalar=bcol[:, bias, m:m + 1],
                                         in1=xres[:, m], op0=ALU.add, op1=ALU.add).then_inc(ready, 1)

            def split_q(i, g):
                group = G * i + g
                split(q_f[:, :], q_hi[:, :], q_lo[:, :], q_ready, qhi_ready, q_split, group + 1)

            def self_product(i, g, first):
                dve.wait_ge(gemm_ready, units(i) + first + UNIT_KSELF + 1)
                dve.wait_ge(q_split, G * i + g + 1)
                dve.scalar_tensor_tensor(out=q_f[:, :], in0=gb[UNIT_KSELF % 2][:, :], scalar=bcol[:, BKSELF, g:g + 1],
                                         in1=q_f[:, :], op0=ALU.add, op1=ALU.mult).then_inc(prod_ready, 1)

            def split_k(i, g):
                dve.wait_ge(khi_ready, G * i + g + 1)
                dve.scalar_tensor_tensor(out=k_lo[:, :], in0=gb[UNIT_K % 2][:, :], scalar=bcol[:, BK, g:g + 1],
                                         in1=k_hi[:, :].bitcast(F32), op0=ALU.add, op1=ALU.subtract
                                         ).then_inc(k_split, 1)

            def take_results(i, g):
                group = G * i + g
                dve.wait_ge(probs_used, TILES * group + TILES)
                dve.wait_ge(eself_ready, group + 1)
                wait(dve, at_lo, group)
                dve.tensor_tensor(den[:, :], dn[:, :], nself[:, :], ALU.add).then_inc(den_ready, 1)
                dve.wait_ge(wself_ready, group + 1)
                dve.tensor_tensor(num[:, :], pv[:, :], vself[:, g % 2], ALU.add).then_inc(fin_read, 1)

            def normalise(i, g):
                group = G * i + g
                dve.wait_ge(den_ready, group + 1)
                dve.reciprocal(den[:, :], den[:, :]).then_inc(recip_ready, 1)
                dve.wait_ge(fin_read, group + 1)
                dve.wait_ge(recip_ready, group + 1)
                dve.tensor_tensor(num[:, :], num[:, :], den[:, :], ALU.mult).then_inc(norm_ready, 1)
                dve.wait_ge(norm_ready, group + 1)
                dve.tensor_scalar(at_s[:, 0, g], num[:, :], bcol[:, BV, g:g + 1], None, ALU.add).then_inc(at_hi, 1)
                dve.wait_ge(at_hi, group + 1)
                dve.scalar_tensor_tensor(out=at_s[:, 1, g], in0=num[:, :], scalar=bcol[:, BV, g:g + 1],
                                         in1=at_s[:, 0, g].bitcast(F32), op0=ALU.add, op1=ALU.subtract
                                         ).then_inc(at_lo, 1)

            def body(i, last):
                dve.wait_ge(b1_in, 16 * (i + 1))
                wait(dve, out_kept, 16 * C * i)
                for m in range(C):
                    sum_x2(i, m)
                split_q(i, 0)
                self_product(i, 0, U_PROJ0)
                split_k(i, 0)
                l0_unit = units(i) + U_L0
                for g in range(G):
                    group, first = G * i + g, U_PROJ + C * g
                    if g:
                        take_results(i, g - 1)
                    wait(dve, mxrep_ready, group)
                    for t in range(TILES):
                        c, h0 = t // 2, 2 * (t % 2)
                        dve.wait_ge(s_ready, 2 * TILES * group + t + 1)
                        dve.tensor_reduce(mx[:, c, h0:h0 + 2], sc[t % 2][:, :, :], AX.X, ALU.max).then_inc(red_ready, 1)
                        if t == C - 1:
                            if g < G - 1:
                                split_q(i, g + 1)
                            elif not last:
                                sum_x1(i + 1, 0, l0_unit)
                                x_lo_block(i + 1, 2)
                    dve.wait_ge(red_ready, TILES * (group + 1))
                    dve.tensor_copy(mx_rep.rearrange("p (a d) -> p a d", d=DH),
                                    mx[:, :, :].rearrange("p c (h o) -> p (c h) o", o=1)
                                    .to_broadcast([P, C * HG, DH])).then_inc(mxrep_ready, 1)
                    if g < G - 1:
                        self_product(i, g + 1, first)
                    elif not last:
                        sum_x1(i + 1, 1, l0_unit)
                        x_lo_block(i + 1, 3)
                    dve.wait_ge(mt_ready, group + 1)
                    dve.wait_ge(nself_ready, group + 1)
                    dve.scalar_tensor_tensor(out=negm[:, :], in0=pv[:, :], scalar=-1.0, in1=nself[:, :],
                                             op0=ALU.mult, op1=ALU.min).then_inc(negm_ready, 1)
                    if g < G - 1:
                        split_k(i, g + 1)
                    elif not last:
                        sum_x1(i + 1, 2, l0_unit)
                        sum_x1(i + 1, 3, l0_unit)
                    if g == G - 2 and not last:
                        for kc in range(C):
                            t_lo_block(i + 1, kc)
                        for m in range(2):
                            x_lo_block(i + 1, m)
                    if g:
                        normalise(i, g - 1)
                take_results(i, G - 1)
                normalise(i, G - 1)
                u_o = units(i) + U_L0 + (0 if last else C)
                for m in range(C):
                    add_to_xres(u_o, m, BO, x3_sum)
                    split(xres[:, m], x2_s[:, 0, m], x2_s[:, 1, m], x3_sum, x3_hi, x3_lo, C * i + m + 1)
                dve.wait_ge(b3_in, 16 * (i + 1))
                for m in range(C):
                    add_to_xres(u_o + C, m, B3, out_ready)

            dve.wait_ge(consts_in, 13 * 16)
            dve.tensor_copy(len_f[:, :], len_i[:, :]).then_inc(mask_made, 1)
            dve.memset(xres[0:1, 2, :], 1.0).then_inc(mask_made, 1)
            dve.wait_ge(mask_made, 2)
            dve.tensor_scalar(xres[0:B, 1, :], xres[0:B, 0, :], len_f[:, 0:1], MASKED, ALU.is_ge, ALU.mult
                              ).then_inc(mask_made, 1)
            dve.wait_ge(w_hi, 1)
            dve.tensor_tensor(bvs[:, 1], bvec[:, :, :].rearrange("p v c -> p c v"), bvs[:, 0].bitcast(F32),
                              ALU.subtract).then_inc(w_lo, 1)
            for w, dst in enumerate((wq_s, wk_s, wv_s, wo_s)):
                for kc in range(C):
                    lo(dst[:, 1, kc], dst[:, 0, kc], kc, w_hi, 1 + C * w + kc + 1, w_lo)
                if w == 1:
                    for n, which, vec in ((0, BQ, 0), (1, BKSELF, 0), (1, BK, 1)):
                        dve.wait_ge(bias_mm, n + 1)
                        dve.tensor_tensor(bcol[:, which], gb[n][:, 0:2 * C].rearrange("p (c v) -> p v c", v=2)[:, vec],
                                          bcol[:, which], ALU.add).then_inc(bias_ready, 1)
            for kc in range(C):
                t_lo_block(0, kc)
            for m in range(2):
                x_lo_block(0, m)
            sum_x1(0, 0, 0)
            x_lo_block(0, 2)
            sum_x1(0, 1, 0)
            x_lo_block(0, 3)
            sum_x1(0, 2, 0)
            sum_x1(0, 3, 0)
            dve.wait_ge(mask_kept, 32)
            body(0, False)
            with dve.Fori(1, B - 1) as i:
                body(i, False)
            body(B - 1, True)


def kernel(**inputs):
    import numpy as np
    import concourse.bacc as bacc
    from concourse.bass_utils import run_bass_kernel_spmd

    def arr(name):
        return np.asarray(inputs[name])

    def stationary(w):
        n = w.shape[0]
        return w.reshape(n, C, P, C, P).transpose(0, 3, 2, 1, 4).reshape(n, C, P, D)

    def transposed(w):
        return w.transpose(0, 2, 1).reshape(w.shape[0], C, P, D)

    def column(b):
        return b.reshape(-1, C, P).transpose(0, 2, 1)

    x, weight = arr("x"), arr("L1_cond_weight")
    consts = np.concatenate([np.eye(P), np.kron(np.eye(HG), np.ones((DH, DH))), np.ones((P, DH))], 1)
    data = {
        "x_blk": stationary(x), "xT": transposed(x), "Tt": transposed(arr("L0_cond_T")),
        "w1_blk": stationary(weight.transpose(0, 2, 1)), "b1": column(arr("L1_cond_bias")),
        "seqT": transposed(arr("fside_BxSxS_0")),
        "wq": arr("L2_cond_Wq").reshape(C, P, D), "wk": arr("L2_cond_Wk").reshape(C, P, D),
        "wv": arr("L2_cond_Wv").reshape(C, P, D), "wo": arr("L2_cond_Wo").reshape(C, P, D),
        "bq": column(arr("L2_cond_bq"))[0], "bk": column(arr("L2_cond_bk"))[0],
        "bv": column(arr("L2_cond_bv"))[0], "bo": column(arr("L2_cond_bo"))[0],
        "b_prev": column(arr("L2_cond_b_prev"))[0], "b_self": column(arr("L2_cond_b_self"))[0],
        "w3_blk": stationary(arr("L3_cond_W")), "b3": column(arr("L3_cond_b")),
        "steps": arr("itok_B_1_98").reshape(1, B), "subjects": arr("itok_B_0_7").reshape(1, B),
        "lengths": arr("itok_B_18_1004").reshape(B, 1), "cats": arr("itok_B_0_30").reshape(1, B),
        "consts": consts.astype(np.float32),
        "iota": np.tile(np.arange(D, dtype=np.float32), (B, 1)),
    }
    nc = bacc.Bacc("TRN2", target_bir_lowering=False, num_devices=1)
    arrays, args = {}, []
    for name, a in data.items():
        a = np.ascontiguousarray(a)
        arrays[f"in_{name}"] = a
        args.append(nc.dram_tensor(f"in_{name}", a.shape, mybir.dt.from_np(a.dtype), kind="ExternalInput").ap())
    out = nc.dram_tensor("out_t", (B, C, P, D), F32, kind="ExternalOutput").ap()
    build(nc, *args, out)
    r = run_bass_kernel_spmd(nc, [arrays], core_ids=[0])
    return r.results[0]["out_t"].reshape(B, D, D).transpose(0, 2, 1)
```

```python
from contextlib import ExitStack

import concourse.bass as bass
from concourse import mybir

F32 = mybir.dt.float32
F32R = mybir.dt.float32r
I32 = mybir.dt.int32
ALU = mybir.AluOpType
ACT = mybir.ActivationFunctionType
AX = mybir.AxisListType

P = 128
B = 8
D = 512
C = D // P
DH = 32
G = 4
HG = P // DH
SCALE = float(DH) ** -0.5
MASKED = -1e30
ROW_MASK = 3 * DH
ROW_MAX = 3 * DH + 1
K_MAX = 3 * DH + 1
K_ALL = 3 * DH + 2

RAW_SETUP = 4
RAW_L0 = 3
RAW_BODY = 6
UNITS_L0 = C
UNITS_BODY = 9 * C
U_L1, U_PROJ0, U_V, U_PROJ, U_L0 = 0, C, 2 * C, 3 * C, 6 * C
UNIT_Q, UNIT_K, UNIT_KSELF, UNIT_VSELF = range(4)
TILES = 2 * C


def build(nc, x_blk, xT, Tt, w1_blk, b1, seqT, wq, wk, wv, wo, bq, bk, bv, bo, b_prev, b_self,
          w3_blk, b3, steps, subjects, lengths, cats, consts, iota, out):
    with ExitStack() as ctx:
        def sb(name, shape, dt=F32):
            return ctx.enter_context(nc.sbuf_tensor(name, shape, dt))

        def sem(name):
            return ctx.enter_context(nc.semaphore(name))

        wq_s = sb("wq_s", [P, 2, C, D], F32R)
        wk_s = sb("wk_s", [P, 2, C, D], F32R)
        wv_s = sb("wv_s", [P, 2, C, D], F32R)
        wo_s = sb("wo_s", [P, 2, C, D], F32R)
        kst = sb("kst", [P, 2, HG, D], F32R)
        qst = sb("qst", [P, 2, HG, D], F32R)
        x1h, x1l = kst[:, 0], qst[:, 0]
        ts_s = sb("ts_s", [P, 2, C, D], F32R)
        x2_s = sb("x2_s", [P, 2, C, D], F32R)
        at_s = sb("at_s", [P, 2, C, D], F32R)
        xres = sb("xres", [P, C, D])
        wblk = sb("wblk", [P, 2, 2, D], F32R)
        raw = sb("raw", [P, C, D])
        v_sb = sb("v_sb", [P, C, D])
        probs = sb("probs", [P, 2, 2, D])
        q_f = sb("q_f", [P, D])
        q_hi = sb("q_hi", [P, D], F32R)
        q_lo = sb("q_lo", [P, D], F32R)
        k_hi = sb("k_hi", [P, D], F32R)
        k_lo = sb("k_lo", [P, D], F32R)
        vself = sb("vself", [P, 2, D])
        nself = sb("nself", [P, D])
        negm = sb("negm", [P, D], F32R)
        mx_rep = negm[:, :].bitcast(F32)
        num = sb("num", [P, D])
        den = sb("den", [P, D])
        mx = sb("mx", [P, C, HG])
        cst = sb("cst", [P, 2 * P + DH])
        ident, blocks, ones = cst[:, 0:P], cst[:, P:2 * P], cst[:, 2 * P:]
        bcol = sb("bcol", [P, 7, C])
        BQ, BKSELF, BK, BV, BO, B1, B3 = range(7)
        bvec = sb("bvec", [P, 2, C])
        bvs = sb("bvs", [P, 2, C, 2], F32R)
        idx = sb("idx", [1, 3, B], I32)
        len_i = sb("len_i", [B, 1], I32)
        len_f = sb("len_f", [B, 1])
        masks = nc.dram_tensor("masks", (B + 1, D), F32, kind="Internal").ap()

        gb = [ctx.enter_context(nc.psum_tensor(f"gb{n}", [P, D], F32)) for n in range(2)]
        sc = [ctx.enter_context(nc.psum_tensor(f"sc{n}", [P, 2, D], F32)) for n in range(2)]
        pv = ctx.enter_context(nc.psum_tensor("pv", [P, D], F32))
        dn = ctx.enter_context(nc.psum_tensor("dn", [P, D], F32))

        consts_in, mask_made, mask_kept = sem("consts_in"), sem("mask_made"), sem("mask_kept")
        w_hi, w_lo = sem("w_hi"), sem("w_lo")
        bias_mm, bias_ready = sem("bias_mm"), sem("bias_ready")
        raw_in = [sem(f"raw_in{s}") for s in range(C)]
        w1_hi, w1_lo = sem("w1_hi"), sem("w1_lo")
        xb_hi, xb_lo = sem("xb_hi"), sem("xb_lo")
        w3_hi, w3_lo = sem("w3_hi"), sem("w3_lo")
        t_hi, t_lo = sem("t_hi"), sem("t_lo")
        sq_hi, sq_lo = sem("sq_hi"), sem("sq_lo")
        gemm_ready = sem("gemm_ready")
        x1_sum, x1_hi, x1_lo = sem("x1_sum"), sem("x1_hi"), sem("x1_lo")
        x2_part, x2_sum, x2_hi, x2_lo = sem("x2_part"), sem("x2_sum"), sem("x2_hi"), sem("x2_lo")
        x3_sum, x3_hi, x3_lo = sem("x3_sum"), sem("x3_hi"), sem("x3_lo")
        out_ready, out_kept = sem("out_ready"), sem("out_kept")
        b1_in, b3_in = sem("b1_in"), sem("b3_in")
        q_ready, qhi_ready, q_split = sem("q_ready"), sem("qhi_ready"), sem("q_split")
        prod_ready, vself_ready, v_ready = sem("prod_ready"), sem("vself_ready"), sem("v_ready")
        khi_ready, k_split = sem("khi_ready"), sem("k_split")
        qst_in = [sem(f"qst_in{s}") for s in range(2)]
        kst_in = [sem(f"kst_in{s}") for s in range(2)]
        s_ready, red_ready = sem("s_ready"), sem("red_ready")
        mxrep_ready, mt_ready = sem("mxrep_ready"), sem("mt_ready")
        ss_ready, nself_ready = sem("ss_ready"), sem("nself_ready")
        negm_ready, negm_in = sem("negm_ready"), sem("negm_in")
        arg_ready, eself_ready, wself_ready = sem("arg_ready"), sem("eself_ready"), sem("wself_ready")
        probs_ready, probs_used = sem("probs_ready"), sem("probs_used")
        taken = sem("taken")
        den_ready, num_ready = sem("den_ready"), sem("num_ready")
        recip_ready, norm_ready, at_hi, at_lo = sem("recip_ready"), sem("norm_ready"), sem("at_hi"), sem("at_lo")

        def wait(eng, s, value):
            if not (isinstance(value, int) and value <= 0):
                eng.wait_ge(s, value)

        def units(i):
            return UNITS_L0 + UNITS_BODY * i

        def raws(i):
            return RAW_SETUP + RAW_L0 + RAW_BODY * i

        def raw_shared(w, n):
            return n, w + 1

        def raw_l0(i, n):
            return n % C, (RAW_SETUP if isinstance(i, int) and i == 0 else raws(i - 1) + 2) + n // C + 1

        def raw_w1(i, m):
            return m, raws(i) + 1

        def raw_seq(i, kc):
            return kc, raws(i) + 2

        def raw_w3(i, m, last):
            return m, raws(i) + (3 if last else RAW_BODY)

        def q_filled(i, g):
            return 16 * ((2 * i + g // 2 + 1) * 3 * HG + i + 1)

        def k_filled(i, g):
            return 16 * ((2 * i + g // 2 + 1) * 3 * HG + 2 * (i + 1))

        def cols(m):
            return slice(P * m, P * m + P)

        block = ctx.enter_context(nc.Block())

        @block.sync
        def _(sp):
            def flat(src):
                return src.rearrange("a p n -> (a p) n")

            def load(src, slot_count, used, value):
                slot, _ = slot_count
                wait(sp, used, value)
                sp.dma_start(raw[:, slot], src).then_inc(raw_in[slot], 16)

            for dst, src in ((cst[:, :], consts), (bvec[:, 0, :], b_self), (bvec[:, 1, :], b_prev),
                             (bcol[:, BQ], bq), (bcol[:, BKSELF], bk), (bcol[:, BK], bk),
                             (bcol[:, BV], bv), (bcol[:, BO], bo),
                             (idx[0:1, 0, :], steps), (idx[0:1, 1, :], subjects), (idx[0:1, 2, :], cats),
                             (len_i[:, :], lengths), (xres[0:B, 0, :], iota)):
                sp.dma_start(dst, src).then_inc(consts_in, 16)

            def index(which, i, least, most):
                return sp.value_load(idx[0:1, which, bass.ds(i, 1)], min_val=least, max_val=most)

            def load_t(i, used, value):
                t = index(0, i, 1, 100) - 1
                for n in range(C):
                    load(flat(Tt[bass.ds(t, 1), n]), raw_l0(i, n), used, value + n + 1)

            def load_x(i):
                for n in range(C, 3 * C):
                    m = (n - C) // 2
                    src = flat((x_blk if n % 2 == 0 else xT)[bass.ds(i, 1), m])
                    if n < 2 * C:
                        load(src, raw_l0(i, n), t_lo, C * i + n - C + 1)
                    else:
                        load(src, raw_l0(i, n), (xb_lo, x1_lo)[n % 2], C * i + m - 2 + 1)

            def load_w1(i):
                s = index(1, i, 0, 7)
                wait(sp, x2_part, C * i)
                sp.dma_start(bcol[:, B1], flat(b1[bass.ds(s, 1)])).then_inc(b1_in, 16)
                for m in range(C):
                    if isinstance(i, int) and i == 0:
                        load(flat(w1_blk[bass.ds(s, 1), m]), raw_w1(i, m), (xb_lo, x1_lo)[m % 2], 2 + m // 2 + 1)
                    else:
                        load(flat(w1_blk[bass.ds(s, 1), m]), raw_w1(i, m), w3_lo, C * (i - 1) + m + 1)

            def fill(stack, s, parts, filled):
                for n, part in parts:
                    for h in range(HG):
                        sp.dma_start(stack[DH * n:DH * n + DH, s, h].bitcast(F32),
                                     part[DH * h:DH * h + DH, :].bitcast(F32)).then_inc(filled, 16)

            def fill_row(stack, row, s, source, filled):
                sp.dma_start(stack[row:row + 1, s].bitcast(F32),
                             source.rearrange("a (o n) -> a o n", o=1).to_broadcast([1, HG, D])).then_inc(filled, 16)

            def fill_q(i, g):
                s = g % 2
                sp.wait_ge(q_split, G * i + g + 1)
                if g == 0:
                    sp.wait_ge(x2_sum, C * (i + 1))
                if g < 2:
                    fill_row(qst, ROW_MASK, s, masks[B:B + 1, :], qst_in[s])
                fill(qst, s, ((0, q_hi), (1, q_lo), (2, q_hi)), qst_in[s])

            def fill_k(i, g):
                s = g % 2
                if g < 2:
                    fill_row(kst, ROW_MASK, s, masks[bass.ds(i, 1), :], kst_in[s])
                    fill_row(kst, ROW_MAX, s, masks[B:B + 1, :], kst_in[s])
                sp.wait_ge(khi_ready, G * i + g + 1)
                fill(kst, s, ((0, k_hi), (1, k_hi)), kst_in[s])
                sp.wait_ge(k_split, G * i + g + 1)
                fill(kst, s, ((2, k_lo),), kst_in[s])

            def load_seq(i, kc):
                load(flat(seqT[bass.ds(i, 1), kc]), raw_seq(i, kc), w1_lo, C * i + kc + 1)

            def body(i, last):
                for kc in range(2, C):
                    load_seq(i, kc)
                fill_q(i, 0)
                fill_k(i, 0)
                if not last:
                    load_t(i + 1, sq_lo, C * i)
                for g in range(1, G):
                    fill_q(i, g)
                    fill_k(i, g)
                if not last:
                    load_x(i + 1)
                c = index(2, i, 0, 31)
                wait(sp, out_ready, C * i)
                sp.dma_start(bcol[:, B3], flat(b3[bass.ds(c, 1)])).then_inc(b3_in, 16)
                for m in range(C):
                    used, value = ((sq_lo, C * i + m + 1) if last
                                   else ((xb_lo, x1_lo)[m % 2], C * (i + 1) + 2 + m // 2 + 1))
                    load(flat(w3_blk[bass.ds(c, 1), m]), raw_w3(i, m, last), used, value)
                if not last:
                    load_w1(i + 1)
                for m in range(C):
                    if m == C - 1 and not last:
                        load_seq(i + 1, 0)
                        load_seq(i + 1, 1)
                    if m == 0:
                        continue
                    sp.wait_ge(out_ready, C * i + m + 1)
                    for block_m in ((1, 0) if m == 1 else (m,)):
                        sp.dma_start(flat(out[bass.ds(i, 1), block_m]), xres[:, block_m]).then_inc(out_kept, 16)

            for w, src in enumerate((wq, wk, wv, wo)):
                for n in range(C):
                    load(src[n], raw_shared(w, n), w_lo, 1 + C * (w - 1) + n + 1 if w else 0)
            sp.wait_ge(consts_in, 13 * 16)
            load_t(0, w_lo, 1 + 3 * C)
            sp.wait_ge(mask_made, 3)
            sp.dma_start(masks[0:B, :], xres[0:B, 1, :]).then_inc(mask_kept, 16)
            sp.dma_start(masks[B:B + 1, :], xres[0:1, 2, :]).then_inc(mask_kept, 16)
            load_x(0)
            load_w1(0)
            load_seq(0, 0)
            load_seq(0, 1)
            sp.wait_ge(mask_kept, 32)
            body(0, False)
            with sp.Fori(1, B - 1) as i:
                body(i, False)
            body(B - 1, True)
            sp.wait_ge(out_kept, 16 * C * B)

        @block.tensor
        def _(pe):
            def product(dst, lhs, rhs, start, stop):
                pe.matmul(dst, lhs(0), rhs(0), start=start, stop=False)
                pe.matmul(dst, lhs(0), rhs(1), start=False, stop=False)
                return pe.matmul(dst, lhs(1), rhs(0), start=False, stop=stop)

            def chunk(m, kc, lhs, rhs, emptied, bank=None):
                if kc == 0:
                    wait(pe, *emptied)
                last = product(gb[m % 2][:, :] if bank is None else bank, lhs, rhs, kc == 0, kc == C - 1)
                if kc == C - 1:
                    last.then_inc(gemm_ready, 1)

            def l0(i, m, kc, before):
                if kc == 0:
                    pe.wait_ge(xb_lo, C * i + m + 1)
                if m == 0:
                    pe.wait_ge(t_lo, C * i + kc + 1)
                chunk(m, kc, lambda h: wblk[:, m % 2, h, cols(kc)], lambda h: ts_s[:, h, kc],
                      before[m] if m < 2 else (x1_sum, C * i + m - 1))

            def l1(i, m, kc):
                if kc == 0:
                    pe.wait_ge(w1_lo, C * i + m + 1)
                if m == 0:
                    pe.wait_ge(x1_lo, C * i + kc + 1)
                first = isinstance(i, int) and i == 0
                chunk(m, kc, lambda h: wblk[:, m % 2, h, cols(kc)], lambda h: (x1h, x1l)[h][:, kc],
                      (x2_part, C * i + m - 1) if m >= 2 else
                      (x1_sum, m + 3) if first else (out_ready, C * (i - 1) + m + 3))

            def projection(i, g, m, kc):
                if g == 0 and m == UNIT_Q:
                    pe.wait_ge(sq_lo, C * i + kc + 1)
                if g == 0 and m == UNIT_K:
                    pe.wait_ge(x2_lo, C * i + kc + 1)
                w = (wq_s, wk_s, wk_s, wv_s)[m]
                rhs = x2_s if m == UNIT_K else ts_s
                if m < 2:
                    emptied = ((x2_part, C * i + m + 3) if g == 0 else (v_ready, C * i + m + 3) if g == 1
                               else ((prod_ready, vself_ready)[m], G * i + g))
                else:
                    emptied = (qhi_ready, k_split)[m % 2], G * i + g + 1
                chunk(m, kc, lambda h: w[:, h, kc, cols(g)], lambda h: rhs[:, h, kc], emptied)

            def values(i, m, kc):
                chunk(m, kc, lambda h: x2_s[:, h, kc, cols(m)], lambda h: wv_s[:, h, kc],
                      (v_ready, C * i + m - 1) if m >= 2 else ((prod_ready, vself_ready)[m], G * i + 1))

            def l2_out(i, last, m, kc):
                if m == 0:
                    pe.wait_ge(at_lo, G * i + kc + 1)
                chunk(m, kc, lambda h: wo_s[:, h, kc, cols(m)], lambda h: at_s[:, h, kc],
                      (probs_ready, TILES * G * (i + 1)) if m == 2 else (x3_sum, C * i + 2) if m == 3 else
                      ((prod_ready, vself_ready)[m], G * i + G) if last else (x1_sum, C * (i + 1) + m + 3),
                      sc[0][:, 0] if m == 2 else None)

            def l3(i, m, kc):
                if kc == 0:
                    pe.wait_ge(w3_lo, C * i + m + 1)
                if m == 0:
                    pe.wait_ge(x3_lo, C * i + kc + 1)
                chunk(m, kc, lambda h: wblk[:, m % 2, h, cols(kc)], lambda h: x2_s[:, h, kc],
                      (out_ready, C * i + m - 1) if m >= 2 else (x3_sum, C * i + (1, 4)[m]))

            def out_order(step):
                for m, kc in ([(m, kc) for m in range(C - 1) for kc in range(C - 1)]
                              + [(m, C - 1) for m in range(C - 1)] + [(C - 1, kc) for kc in range(C)]):
                    step(m, kc)

            def l3_order(step):
                for m, kc in ([(0, 0), (0, 1), (0, 2), (1, 0), (1, 1), (0, 3), (1, 2), (1, 3)]
                              + [(m, kc) for m in range(2, C) for kc in range(C)]):
                    step(m, kc)

            def score_tile(t, lhs, rhs):
                for j in range(2):
                    mm = pe.matmul(sc[t % 2][:, j], lhs(j), rhs(j), start=True, stop=True)
                mm.then_inc(s_ready, 1)

            def body(i, last):
                for m in range(C):
                    for kc in range(C):
                        l1(i, m, kc)
                for m in range(C):
                    for kc in range(C):
                        projection(i, 0, m, kc)
                for m in range(C):
                    for kc in range(C):
                        values(i, m, kc)

                for g in range(G):
                    slot, group = g % 2, G * i + g
                    before_l0 = ((prod_ready, G * i + G), (vself_ready, G * i + G))

                    def beside(n):
                        if g < G - 1:
                            projection(i, g + 1, n // C, n % C)
                        elif not last:
                            l0(i + 1, n // C, n % C, before_l0)

                    pe.wait_ge(qst_in[slot], q_filled(i, g))
                    pe.wait_ge(kst_in[slot], k_filled(i, g))
                    for t in range(TILES):
                        c, h0 = t // 2, 2 * (t % 2)
                        if t < 2:
                            wait(pe, probs_ready, TILES * group - 1 + t)
                            if g == 0:
                                wait(pe, x3_sum, C * i)
                        else:
                            pe.wait_ge(red_ready, TILES * group + t - 1)
                        score_tile(t, lambda j: qst[0:K_MAX, slot, h0 + j, cols(c)],
                                   lambda j: kst[0:K_MAX, slot, h0 + j, :])
                        beside(t)
                        if t == C - 1:
                            pe.wait_ge(prod_ready, group + 1)
                            wait(pe, taken, group)
                            pe.matmul(dn[:, :], blocks, q_f[:, :], start=True, stop=True).then_inc(ss_ready, 1)
                    for n in range(8, 11):
                        beside(n)
                    pe.wait_ge(mxrep_ready, group + 1)
                    for c in range(C):
                        mm = pe.transpose(pv[:, cols(c)], mx_rep[:, cols(c)], ident)
                    mm.then_inc(mt_ready, 1)
                    for n in range(11, 16):
                        beside(n)

                    def prob_scores(t):
                        c, h0 = t // 2, 2 * (t % 2)
                        score_tile(t, lambda j: kst[0:K_ALL, slot, h0 + j, cols(c)],
                                   lambda j: qst[0:K_ALL, slot, h0 + j, :])

                    pe.wait_ge(negm_in, 16 * (group + 1))
                    pe.wait_ge(nself_ready, group + 1)
                    if g == 0:
                        pe.wait_ge(v_ready, C * i + C)
                    for t in range(2):
                        pe.wait_ge(red_ready, TILES * group + TILES - 1 + t)
                        prob_scores(t)
                    for t in range(TILES):
                        c, h0 = t // 2, 2 * (t % 2)
                        pe.wait_ge(probs_ready, TILES * group + t + 1)
                        for j in range(2):
                            row = DH * (h0 + j)
                            pe.matmul(pv[row:row + DH, :], v_sb[:, c, P * g + row:P * g + row + DH], probs[:, t % 2, j],
                                      start=(c == 0), stop=(c == C - 1), tile_position=(0, row))
                        for j in range(2):
                            row = (DH * (h0 + j) + P // 2) % P
                            mm = pe.matmul(dn[row:row + DH, :], ones, probs[:, t % 2, j], start=(c == 0),
                                           stop=(c == C - 1), tile_position=(0, row))
                        mm.then_inc(probs_used, 1)
                        if t + 2 < TILES:
                            prob_scores(t + 2)

                out_order(lambda m, kc: l2_out(i, last, m, kc))
                l3_order(lambda m, kc: l3(i, m, kc))

            pe.wait_ge(w_lo, 1 + 2 * C)
            for n, w in enumerate((wq_s, wk_s)):
                for m in range(C):
                    for kc in range(C):
                        mm = product(gb[n][:, 2 * m:2 * m + 2], lambda h: w[:, h, kc, cols(m)],
                                     lambda h: bvs[:, h, kc], kc == 0, kc == C - 1)
                mm.then_inc(bias_mm, 1)
            for m in range(C):
                for kc in range(C):
                    l0(0, m, kc, ((bias_ready, 1), (bias_ready, 3)))
            pe.wait_ge(w_lo, 1 + 4 * C)
            pe.wait_ge(consts_in, 13 * 16)
            body(0, False)
            with pe.Fori(1, B - 1) as i:
                body(i, False)
            body(B - 1, True)

        @block.scalar
        def _(act):
            def hi(dst, slot_count, ready):
                slot, count = slot_count
                act.wait_ge(raw_in[slot], 16 * count)
                act.activation(dst, raw[:, slot], ACT.Copy).then_inc(ready, 1)

            def evacuate(dst, i, unit, bias, ready):
                act.wait_ge(gemm_ready, units(i) + unit + 1)
                act.activation(dst, gb[unit % 2][:, :], ACT.Identity, bias=bias).then_inc(ready, 1)

            def project_qk(i, g, first):
                evacuate(q_f[:, :], i, first + UNIT_Q, bcol[:, BQ, g:g + 1], q_ready)
                evacuate(q_hi[:, :], i, first + UNIT_Q, bcol[:, BQ, g:g + 1], qhi_ready)
                evacuate(k_hi[:, :], i, first + UNIT_K, bcol[:, BK, g:g + 1], khi_ready)

            def project_v(i, g, first):
                act.wait_ge(gemm_ready, units(i) + first + UNIT_VSELF + 1)
                wait(act, num_ready, G * i + g - 1)
                act.activation(vself[:, g % 2], gb[UNIT_VSELF % 2][:, :], ACT.Copy).then_inc(vself_ready, 1)

            def take_results(i, g):
                group = G * i + g
                act.wait_ge(probs_used, TILES * group + TILES)
                wait(act, at_lo, group)
                half = P // 2
                act.activation(den[0:half, :], dn[half:P, :], ACT.Copy)
                act.activation(den[half:P, :], dn[0:half, :], ACT.Copy)
                act.activation(num[:, :], pv[:, :], ACT.Copy).then_inc(taken, 1)

            def body(i, last):
                for m in range(2):
                    act.wait_ge(gemm_ready, units(i) - 2 + m + 1)
                    hi(wblk[:, m % 2, 0], raw_w1(i, m), w1_hi)
                for kc in range(2):
                    hi(ts_s[:, 0, kc], raw_seq(i, kc), sq_hi)
                for m in range(2, C):
                    act.wait_ge(gemm_ready, units(i) + U_L1 + m - 1)
                    hi(wblk[:, m % 2, 0], raw_w1(i, m), w1_hi)
                for kc in range(2, C):
                    hi(ts_s[:, 0, kc], raw_seq(i, kc), sq_hi)
                project_qk(i, 0, U_PROJ0)
                project_v(i, 0, U_PROJ0)
                for m in range(C):
                    act.wait_ge(gemm_ready, units(i) + U_V + m + 1)
                    act.activation(v_sb[:, m], gb[m % 2][:, :], ACT.Copy).then_inc(v_ready, 1)

                for g in range(G):
                    group, first = G * i + g, U_PROJ + C * g
                    if g:
                        take_results(i, g - 1)
                    act.wait_ge(ss_ready, group + 1)
                    wait(act, den_ready, group)
                    act.activation(nself[:, :], dn[:, :], ACT.Copy, scale=-1.0).then_inc(nself_ready, 1)
                    if g < G - 1:
                        project_qk(i, g + 1, first)
                    elif not last:
                        for m in range(2, C):
                            act.wait_ge(gemm_ready, units(i) + U_L0 + m - 1)
                            hi(wblk[:, m % 2, 0], raw_l0(i + 1, C + 2 * m), xb_hi)
                    act.wait_ge(negm_ready, group + 1)
                    act.dma_start(qst[ROW_MAX:ROW_MAX + 1, g % 2].bitcast(F32), negm[0:P:DH, :].bitcast(F32)
                                  ).then_inc(negm_in, 16)
                    if g < G - 1:
                        project_v(i, g + 1, first)
                    for t in range(TILES):
                        act.wait_ge(s_ready, 2 * TILES * group + TILES + t + 1)
                        wait(act, probs_used, TILES * group + t - 1)
                        act.activation(probs[:, t % 2], sc[t % 2][:, :, :], ACT.Exp, scale=SCALE
                                       ).then_inc(probs_ready, 1)
                        if t == 1:
                            act.wait_ge(arg_ready, group + 1)
                            act.activation(nself[:, :], nself[:, :], ACT.Exp, scale=SCALE).then_inc(eself_ready, 1)
                        if g == G - 2 and not last:
                            if t < C:
                                hi(ts_s[:, 0, t], raw_l0(i + 1, t), t_hi)
                            elif t >= TILES - 2:
                                m = t - TILES + 2
                                hi(wblk[:, m % 2, 0], raw_l0(i + 1, C + 2 * m), xb_hi)
                take_results(i, G - 1)
                u_out = U_L0 + (0 if last else C)
                for m in range(2):
                    act.wait_ge(gemm_ready, units(i) + (U_L1 + m + 3 if last else U_L0 + m + 3))
                    hi(wblk[:, m % 2, 0], raw_w3(i, m, last), w3_hi)
                for m in range(C):
                    act.wait_ge(x3_sum, C * i + m + 1)
                    act.activation(x2_s[:, 0, m], xres[:, m], ACT.Copy).then_inc(x3_hi, 1)
                for m in range(2, C):
                    act.wait_ge(gemm_ready, units(i) + u_out + C + m - 1)
                    hi(wblk[:, m % 2, 0], raw_w3(i, m, last), w3_hi)

            act.wait_ge(consts_in, 13 * 16)
            act.activation(bvs[:, 0], bvec[:, :, :].rearrange("p v c -> p c v"), ACT.Copy).then_inc(w_hi, 1)
            for w, dst in enumerate((wq_s, wk_s, wv_s, wo_s)):
                for kc in range(C):
                    hi(dst[:, 0, kc], raw_shared(w, kc), w_hi)
            for kc in range(C):
                hi(ts_s[:, 0, kc], raw_l0(0, kc), t_hi)
            for m in range(C):
                if m >= 2:
                    act.wait_ge(gemm_ready, m - 1)
                hi(wblk[:, m % 2, 0], raw_l0(0, C + 2 * m), xb_hi)
            body(0, False)
            with act.Fori(1, B - 1) as i:
                body(i, False)
            body(B - 1, True)

        @block.gpsimd
        def _(pool):
            def lo(dst, hi_part, slot, hi_ready, count, ready):
                pool.wait_ge(hi_ready, count)
                pool.tensor_tensor(dst, raw[:, slot], hi_part.bitcast(F32), ALU.subtract).then_inc(ready, 1)

            def x_lo_block(i, m):
                lo(wblk[:, m % 2, 1], wblk[:, m % 2, 0], (2 * m) % C, xb_hi, C * i + m + 1, xb_lo)

            def split_q(i, g):
                pool.wait_ge(qhi_ready, G * i + g + 1)
                pool.tensor_tensor(q_lo[:, :], q_f[:, :], q_hi[:, :].bitcast(F32), ALU.subtract).then_inc(q_split, 1)

            def add_self(i, g):
                pool.wait_ge(taken, G * i + g + 1)
                pool.tensor_tensor(den[:, :], den[:, :], nself[:, :], ALU.add).then_inc(den_ready, 1)
                pool.wait_ge(wself_ready, G * i + g + 1)
                pool.tensor_tensor(num[:, :], num[:, :], vself[:, g % 2], ALU.add).then_inc(num_ready, 1)

            def body(i, last):
                for m in range(2):
                    lo(wblk[:, m % 2, 1], wblk[:, m % 2, 0], m, w1_hi, C * i + m + 1, w1_lo)
                for kc in range(2):
                    lo(ts_s[:, 1, kc], ts_s[:, 0, kc], kc, sq_hi, C * i + kc + 1, sq_lo)
                for m in range(2, C):
                    lo(wblk[:, m % 2, 1], wblk[:, m % 2, 0], m, w1_hi, C * i + m + 1, w1_lo)
                for kc in range(2, C):
                    lo(ts_s[:, 1, kc], ts_s[:, 0, kc], kc, sq_hi, C * i + kc + 1, sq_lo)
                split_q(i, 0)
                for g in range(G):
                    group = G * i + g
                    if g:
                        add_self(i, g - 1)
                    if g < G - 1:
                        split_q(i, g + 1)
                    elif not last:
                        x_lo_block(i + 1, 2)
                        x_lo_block(i + 1, 3)
                    pool.wait_ge(negm_ready, group + 1)
                    pool.tensor_tensor(nself[:, :], negm[:, :].bitcast(F32), nself[:, :], ALU.subtract
                                       ).then_inc(arg_ready, 1)
                    pool.wait_ge(eself_ready, group + 1)
                    pool.tensor_tensor(vself[:, g % 2], vself[:, g % 2], nself[:, :], ALU.mult
                                       ).then_inc(wself_ready, 1)
                    if g == G - 2 and not last:
                        x_lo_block(i + 1, 0)
                        x_lo_block(i + 1, 1)
                add_self(i, G - 1)
                for m in range(C):
                    lo(wblk[:, m % 2, 1], wblk[:, m % 2, 0], m, w3_hi, C * i + m + 1, w3_lo)

            for m in range(C):
                x_lo_block(0, m)
            body(0, False)
            with pool.Fori(1, B - 1) as i:
                body(i, False)
            body(B - 1, True)

        @block.vector
        def _(dve):
            def lo(dst, hi_part, slot, hi_ready, count, ready):
                dve.wait_ge(hi_ready, count)
                dve.tensor_tensor(dst, raw[:, slot], hi_part.bitcast(F32), ALU.subtract).then_inc(ready, 1)

            def split(src, hi_part, lo_part, summed, hi_ready, lo_ready, count):
                dve.wait_ge(summed, count)
                dve.tensor_copy(hi_part, src).then_inc(hi_ready, 1)
                dve.wait_ge(hi_ready, count)
                dve.tensor_tensor(lo_part, src, hi_part.bitcast(F32), ALU.subtract).then_inc(lo_ready, 1)

            def t_lo_block(i, kc):
                lo(ts_s[:, 1, kc], ts_s[:, 0, kc], kc, t_hi, C * i + kc + 1, t_lo)

            def sum_x1(i, m, unit):
                slot, count = raw_l0(i, C + 2 * m + 1)
                dve.wait_ge(raw_in[slot], 16 * count)
                dve.wait_ge(gemm_ready, unit + m + 1)
                dve.tensor_tensor(raw[:, slot], gb[m % 2][:, :], raw[:, slot], ALU.add).then_inc(x1_sum, 1)
                split(raw[:, slot], x1h[:, m], x1l[:, m], x1_sum, x1_hi, x1_lo, C * i + m + 1)

            def sum_x2(i, m):
                dve.wait_ge(gemm_ready, units(i) + U_L1 + m + 1)
                dve.scalar_tensor_tensor(out=xres[:, m], in0=gb[m % 2][:, :], scalar=bcol[:, B1, m:m + 1],
                                         in1=x1h[:, m].bitcast(F32), op0=ALU.add, op1=ALU.add).then_inc(x2_part, 1)
                dve.wait_ge(x2_part, C * i + m + 1)
                dve.tensor_tensor(xres[:, m], xres[:, m], x1l[:, m].bitcast(F32), ALU.add).then_inc(x2_sum, 1)
                split(xres[:, m], x2_s[:, 0, m], x2_s[:, 1, m], x2_sum, x2_hi, x2_lo, C * i + m + 1)

            def add_to_xres(unit, m, bias, ready, bank=None):
                dve.wait_ge(gemm_ready, unit + m + 1)
                dve.scalar_tensor_tensor(out=xres[:, m], in0=gb[m % 2][:, :] if bank is None else bank, scalar=bcol[:, bias, m:m + 1],
                                         in1=xres[:, m], op0=ALU.add, op1=ALU.add).then_inc(ready, 1)

            def self_product(i, g, first):
                dve.wait_ge(gemm_ready, units(i) + first + UNIT_KSELF + 1)
                dve.wait_ge(q_split, G * i + g + 1)
                dve.scalar_tensor_tensor(out=q_f[:, :], in0=gb[UNIT_KSELF % 2][:, :], scalar=bcol[:, BKSELF, g:g + 1],
                                         in1=q_f[:, :], op0=ALU.add, op1=ALU.mult).then_inc(prod_ready, 1)

            def split_k(i, g):
                dve.wait_ge(khi_ready, G * i + g + 1)
                dve.scalar_tensor_tensor(out=k_lo[:, :], in0=gb[UNIT_K % 2][:, :], scalar=bcol[:, BK, g:g + 1],
                                         in1=k_hi[:, :].bitcast(F32), op0=ALU.add, op1=ALU.subtract
                                         ).then_inc(k_split, 1)

            def normalise(i, g):
                group = G * i + g
                dve.wait_ge(den_ready, group + 1)
                dve.reciprocal(den[:, :], den[:, :]).then_inc(recip_ready, 1)
                dve.wait_ge(num_ready, group + 1)
                dve.wait_ge(recip_ready, group + 1)
                dve.tensor_tensor(num[:, :], num[:, :], den[:, :], ALU.mult).then_inc(norm_ready, 1)
                dve.wait_ge(norm_ready, group + 1)
                dve.tensor_scalar(at_s[:, 0, g], num[:, :], bcol[:, BV, g:g + 1], None, ALU.add).then_inc(at_hi, 1)
                dve.wait_ge(at_hi, group + 1)
                dve.scalar_tensor_tensor(out=at_s[:, 1, g], in0=num[:, :], scalar=bcol[:, BV, g:g + 1],
                                         in1=at_s[:, 0, g].bitcast(F32), op0=ALU.add, op1=ALU.subtract
                                         ).then_inc(at_lo, 1)

            def body(i, last):
                dve.wait_ge(b1_in, 16 * (i + 1))
                wait(dve, out_kept, 16 * C * i)
                for m in range(C):
                    sum_x2(i, m)
                split_k(i, 0)
                self_product(i, 0, U_PROJ0)
                l0_unit = units(i) + U_L0
                for g in range(G):
                    group, first = G * i + g, U_PROJ + C * g
                    wait(dve, mxrep_ready, group)
                    for t in range(TILES):
                        c, h0 = t // 2, 2 * (t % 2)
                        dve.wait_ge(s_ready, 2 * TILES * group + t + 1)
                        dve.tensor_reduce(mx[:, c, h0:h0 + 2], sc[t % 2][:, :, :], AX.X, ALU.max).then_inc(red_ready, 1)
                        if t == C - 1 and g == G - 1 and not last:
                            sum_x1(i + 1, 0, l0_unit)
                    dve.wait_ge(red_ready, TILES * (group + 1))
                    dve.tensor_copy(mx_rep.rearrange("p (a d) -> p a d", d=DH),
                                    mx[:, :, :].rearrange("p c (h o) -> p (c h) o", o=1)
                                    .to_broadcast([P, C * HG, DH])).then_inc(mxrep_ready, 1)
                    if g < G - 1:
                        split_k(i, g + 1)
                    elif not last:
                        sum_x1(i + 1, 1, l0_unit)
                    dve.wait_ge(mt_ready, group + 1)
                    dve.wait_ge(nself_ready, group + 1)
                    dve.scalar_tensor_tensor(out=negm[:, :], in0=pv[:, :], scalar=-1.0, in1=nself[:, :],
                                             op0=ALU.mult, op1=ALU.min).then_inc(negm_ready, 1)
                    if g < G - 1:
                        self_product(i, g + 1, first)
                    elif not last:
                        sum_x1(i + 1, 2, l0_unit)
                        sum_x1(i + 1, 3, l0_unit)
                    if g == G - 2 and not last:
                        for kc in range(C):
                            t_lo_block(i + 1, kc)
                    if g:
                        normalise(i, g - 1)
                normalise(i, G - 1)
                u_o = units(i) + U_L0 + (0 if last else C)
                for m in range(C + 1):
                    if m < C:
                        add_to_xres(u_o, m, BO, x3_sum, sc[0][:, 0] if m == 2 else None)
                    if m:
                        dve.wait_ge(x3_hi, C * i + m)
                        dve.tensor_tensor(x2_s[:, 1, m - 1], xres[:, m - 1], x2_s[:, 0, m - 1].bitcast(F32),
                                          ALU.subtract).then_inc(x3_lo, 1)
                dve.wait_ge(b3_in, 16 * (i + 1))
                for m in range(C):
                    add_to_xres(u_o + C, m, B3, out_ready)

            dve.wait_ge(consts_in, 13 * 16)
            dve.tensor_copy(len_f[:, :], len_i[:, :]).then_inc(mask_made, 1)
            dve.memset(xres[0:1, 2, :], 1.0).then_inc(mask_made, 1)
            dve.wait_ge(mask_made, 2)
            dve.tensor_scalar(xres[0:B, 1, :], xres[0:B, 0, :], len_f[:, 0:1], MASKED, ALU.is_ge, ALU.mult
                              ).then_inc(mask_made, 1)
            dve.wait_ge(w_hi, 1)
            dve.tensor_tensor(bvs[:, 1], bvec[:, :, :].rearrange("p v c -> p c v"), bvs[:, 0].bitcast(F32),
                              ALU.subtract).then_inc(w_lo, 1)
            for w, dst in enumerate((wq_s, wk_s, wv_s, wo_s)):
                for kc in range(C):
                    lo(dst[:, 1, kc], dst[:, 0, kc], kc, w_hi, 1 + C * w + kc + 1, w_lo)
                if w == 1:
                    for n, which, vec in ((0, BQ, 0), (1, BKSELF, 0), (1, BK, 1)):
                        dve.wait_ge(bias_mm, n + 1)
                        dve.tensor_tensor(bcol[:, which], gb[n][:, 0:2 * C].rearrange("p (c v) -> p v c", v=2)[:, vec],
                                          bcol[:, which], ALU.add).then_inc(bias_ready, 1)
            for kc in range(C):
                t_lo_block(0, kc)
            for m in range(C):
                sum_x1(0, m, 0)
            dve.wait_ge(mask_kept, 32)
            body(0, False)
            with dve.Fori(1, B - 1) as i:
                body(i, False)
            body(B - 1, True)


def kernel(**inputs):
    import numpy as np
    import concourse.bacc as bacc
    from concourse.bass_utils import run_bass_kernel_spmd

    def arr(name):
        return np.asarray(inputs[name])

    def stationary(w):
        n = w.shape[0]
        return w.reshape(n, C, P, C, P).transpose(0, 3, 2, 1, 4).reshape(n, C, P, D)

    def transposed(w):
        return w.transpose(0, 2, 1).reshape(w.shape[0], C, P, D)

    def column(b):
        return b.reshape(-1, C, P).transpose(0, 2, 1)

    x, weight = arr("x"), arr("L1_cond_weight")
    consts = np.concatenate([np.eye(P), np.kron(np.eye(HG), np.ones((DH, DH))), np.ones((P, DH))], 1)
    data = {
        "x_blk": stationary(x), "xT": transposed(x), "Tt": transposed(arr("L0_cond_T")),
        "w1_blk": stationary(weight.transpose(0, 2, 1)), "b1": column(arr("L1_cond_bias")),
        "seqT": transposed(arr("fside_BxSxS_0")),
        "wq": arr("L2_cond_Wq").reshape(C, P, D), "wk": arr("L2_cond_Wk").reshape(C, P, D),
        "wv": arr("L2_cond_Wv").reshape(C, P, D), "wo": arr("L2_cond_Wo").reshape(C, P, D),
        "bq": column(arr("L2_cond_bq"))[0], "bk": column(arr("L2_cond_bk"))[0],
        "bv": column(arr("L2_cond_bv"))[0], "bo": column(arr("L2_cond_bo"))[0],
        "b_prev": column(arr("L2_cond_b_prev"))[0], "b_self": column(arr("L2_cond_b_self"))[0],
        "w3_blk": stationary(arr("L3_cond_W")), "b3": column(arr("L3_cond_b")),
        "steps": arr("itok_B_1_98").reshape(1, B), "subjects": arr("itok_B_0_7").reshape(1, B),
        "lengths": arr("itok_B_18_1004").reshape(B, 1), "cats": arr("itok_B_0_30").reshape(1, B),
        "consts": consts.astype(np.float32),
        "iota": np.tile(np.arange(D, dtype=np.float32), (B, 1)),
    }
    nc = bacc.Bacc("TRN2", target_bir_lowering=False, num_devices=1)
    arrays, args = {}, []
    for name, a in data.items():
        a = np.ascontiguousarray(a)
        arrays[f"in_{name}"] = a
        args.append(nc.dram_tensor(f"in_{name}", a.shape, mybir.dt.from_np(a.dtype), kind="ExternalInput").ap())
    out = nc.dram_tensor("out_t", (B, C, P, D), F32, kind="ExternalOutput").ap()
    build(nc, *args, out)
    r = run_bass_kernel_spmd(nc, [arrays], core_ids=[0])
    return r.results[0]["out_t"].reshape(B, D, D).transpose(0, 2, 1)
```

```python
from contextlib import ExitStack

import concourse.bass as bass
from concourse import mybir

F32 = mybir.dt.float32
F32R = mybir.dt.float32r
I32 = mybir.dt.int32
ALU = mybir.AluOpType
ACT = mybir.ActivationFunctionType
AX = mybir.AxisListType

P = 128
B = 8
D = 512
C = D // P
DH = 32
G = 4
HG = P // DH
SCALE = float(DH) ** -0.5
MASKED = -1e30
ROW_MASK = 3 * DH
ROW_MAX = 3 * DH + 1
K_MAX = 3 * DH + 1
K_ALL = 3 * DH + 2

RAW_SETUP = 4
RAW_L0 = 3
RAW_BODY = 6
UNITS_L0 = C
UNITS_BODY = 9 * C
U_L1, U_PROJ0, U_V, U_PROJ, U_L0 = 0, C, 2 * C, 3 * C, 6 * C
UNIT_Q, UNIT_K, UNIT_KSELF, UNIT_VSELF = range(4)
TILES = 2 * C


def build(nc, x_blk, xT, Tt, w1_blk, b1, seqT, wq, wk, wv, wo, bq, bk, bv, bo, b_prev, b_self,
          w3_blk, b3, steps, subjects, lengths, cats, consts, iota, out):
    with ExitStack() as ctx:
        def sb(name, shape, dt=F32):
            return ctx.enter_context(nc.sbuf_tensor(name, shape, dt))

        def sem(name):
            return ctx.enter_context(nc.semaphore(name))

        wq_s = sb("wq_s", [P, 2, C, D], F32R)
        wk_s = sb("wk_s", [P, 2, C, D], F32R)
        wv_s = sb("wv_s", [P, 2, C, D], F32R)
        wo_s = sb("wo_s", [P, 2, C, D], F32R)
        kst = sb("kst", [P, 2, HG, D], F32R)
        qst = sb("qst", [P, 2, HG, D], F32R)
        x1h, x1l = kst[:, 0], qst[:, 0]
        ts_s = sb("ts_s", [P, 2, C, D], F32R)
        x2_s = sb("x2_s", [P, 2, C, D], F32R)
        at_s = sb("at_s", [P, 2, C, D], F32R)
        xres = sb("xres", [P, C, D])
        wblk = sb("wblk", [P, 2, 2, D], F32R)
        raw = sb("raw", [P, C, D])
        v_sb = sb("v_sb", [P, C, D])
        probs = sb("probs", [P, 2, 2, D])
        q_f = sb("q_f", [P, D])
        q_hi = sb("q_hi", [P, D], F32R)
        q_lo = sb("q_lo", [P, D], F32R)
        k_hi = sb("k_hi", [P, D], F32R)
        k_lo = sb("k_lo", [P, D], F32R)
        vself = sb("vself", [P, 2, D])
        nself = sb("nself", [P, D])
        negm = sb("negm", [P, D], F32R)
        mx_rep = negm[:, :].bitcast(F32)
        num = sb("num", [P, D])
        den = sb("den", [P, D])
        mx = sb("mx", [P, C, HG])
        cst = sb("cst", [P, 2 * P + DH])
        ident, blocks, ones = cst[:, 0:P], cst[:, P:2 * P], cst[:, 2 * P:]
        bcol = sb("bcol", [P, 7, C])
        BQ, BKSELF, BK, BV, BO, B1, B3 = range(7)
        bvec = sb("bvec", [P, 2, C])
        bvs = sb("bvs", [P, 2, C, 2], F32R)
        idx = sb("idx", [1, 3, B], I32)
        len_i = sb("len_i", [B, 1], I32)
        len_f = sb("len_f", [B, 1])
        masks = nc.dram_tensor("masks", (B + 1, D), F32, kind="Internal").ap()

        gb = [ctx.enter_context(nc.psum_tensor(f"gb{n}", [P, D], F32)) for n in range(2)]
        sc = [ctx.enter_context(nc.psum_tensor(f"sc{n}", [P, 2, D], F32)) for n in range(2)]
        pv = ctx.enter_context(nc.psum_tensor("pv", [P, D], F32))
        dn = ctx.enter_context(nc.psum_tensor("dn", [P, D], F32))

        idx_in, consts_in = sem("idx_in"), sem("consts_in")
        mask_made, mask_kept = sem("mask_made"), sem("mask_kept")
        w_hi, w_lo = sem("w_hi"), sem("w_lo")
        bias_mm, bias_ready = sem("bias_mm"), sem("bias_ready")
        raw_in = [sem(f"raw_in{s}") for s in range(C)]
        w1_hi, w1_lo = sem("w1_hi"), sem("w1_lo")
        xb_hi, xb_lo = sem("xb_hi"), sem("xb_lo")
        w3_hi, w3_lo = sem("w3_hi"), sem("w3_lo")
        t_hi, t_lo = sem("t_hi"), sem("t_lo")
        sq_hi, sq_lo = sem("sq_hi"), sem("sq_lo")
        gemm_ready = sem("gemm_ready")
        x1_sum, x1_hi, x1_lo = sem("x1_sum"), sem("x1_hi"), sem("x1_lo")
        x2_part, x2_sum, x2_hi, x2_lo = sem("x2_part"), sem("x2_sum"), sem("x2_hi"), sem("x2_lo")
        x3_sum, x3_hi, x3_lo = sem("x3_sum"), sem("x3_hi"), sem("x3_lo")
        out_ready, out_kept = sem("out_ready"), [sem(f"out_kept{m}") for m in range(C)]
        b1_in, b3_in = sem("b1_in"), sem("b3_in")
        q_ready, qhi_ready, q_split = sem("q_ready"), sem("qhi_ready"), sem("q_split")
        prod_ready, vself_ready, v_ready = sem("prod_ready"), sem("vself_ready"), sem("v_ready")
        khi_ready, k_split = sem("khi_ready"), sem("k_split")
        qst_in = [sem(f"qst_in{s}") for s in range(2)]
        kst_in = [sem(f"kst_in{s}") for s in range(2)]
        s_ready, red_ready = sem("s_ready"), sem("red_ready")
        mxrep_ready, mt_ready = sem("mxrep_ready"), sem("mt_ready")
        ss_ready, nself_ready = sem("ss_ready"), sem("nself_ready")
        negm_ready, negm_in = sem("negm_ready"), sem("negm_in")
        arg_ready, eself_ready, wself_ready = sem("arg_ready"), sem("eself_ready"), sem("wself_ready")
        probs_ready, probs_used = sem("probs_ready"), sem("probs_used")
        taken = sem("taken")
        den_ready, num_ready = sem("den_ready"), sem("num_ready")
        recip_ready, norm_ready, at_hi, at_lo = sem("recip_ready"), sem("norm_ready"), sem("at_hi"), sem("at_lo")

        def wait(eng, s, value):
            if not (isinstance(value, int) and value <= 0):
                eng.wait_ge(s, value)

        def units(i):
            return UNITS_L0 + UNITS_BODY * i

        def raws(i):
            return RAW_SETUP + RAW_L0 + RAW_BODY * i

        def raw_shared(w, n):
            return n, RAW_L0 + w + 1

        def raw_l0(i, n):
            return n % C, (0 if isinstance(i, int) and i == 0 else raws(i - 1) + 2) + n // C + 1

        def raw_w1(i, m):
            return m, raws(i) + 1

        def raw_seq(i, kc):
            return kc, raws(i) + 2

        def raw_w3(i, m, last):
            return m, raws(i) + (3 if last else RAW_BODY)

        def q_filled(i, g):
            return 16 * ((2 * i + g // 2 + 1) * 3 * HG + (1 if g % 2 else i + 1))

        def k_filled(i, g):
            return 16 * ((2 * i + g // 2 + 1) * 3 * HG + i + 1 + (1 if g % 2 else i + 1))

        def cols(m):
            return slice(P * m, P * m + P)

        block = ctx.enter_context(nc.Block())

        @block.sync
        def _(sp):
            def flat(src):
                return src.rearrange("a p n -> (a p) n")

            def load(src, slot_count, used, value):
                slot, _ = slot_count
                wait(sp, used, value)
                sp.dma_start(raw[:, slot], src).then_inc(raw_in[slot], 16)


            def index(which, i, least, most):
                return sp.value_load(idx[0:1, which, bass.ds(i, 1)], min_val=least, max_val=most)

            def load_t(i, used, value):
                t = index(0, i, 1, 100) - 1
                for n in range(C):
                    load(flat(Tt[bass.ds(t, 1), n]), raw_l0(i, n), used, value + n + 1 if used else 0)

            def load_x(i, first, second):
                halves = ((range(C, 2 * C), first), ((2 * C, 2 * C + 2, 2 * C + 1, 2 * C + 3), second))
                for n in [n for half, wanted in halves if wanted for n in half]:
                    m = (n - C) // 2
                    src = flat((x_blk if n % 2 == 0 else xT)[bass.ds(i, 1), m])
                    if n < 2 * C:
                        load(src, raw_l0(i, n), t_lo, C * i + n - C + 1)
                    else:
                        load(src, raw_l0(i, n), (xb_lo, x1_lo)[n % 2], C * i + m - 2 + 1)

            def load_w1(i):
                s = index(1, i, 0, 7)
                wait(sp, x2_part, C * i)
                sp.dma_start(bcol[:, B1], flat(b1[bass.ds(s, 1)])).then_inc(b1_in, 16)
                for m in range(C):
                    if isinstance(i, int) and i == 0:
                        load(flat(w1_blk[bass.ds(s, 1), m]), raw_w1(i, m), w_lo, 1 + 3 * C + m + 1)
                    else:
                        load(flat(w1_blk[bass.ds(s, 1), m]), raw_w1(i, m), w3_lo, C * (i - 1) + m + 1)

            def fill(stack, s, parts, filled):
                for n, part in parts:
                    for h in range(HG):
                        sp.dma_start(stack[DH * n:DH * n + DH, s, h].bitcast(F32),
                                     part[DH * h:DH * h + DH, :].bitcast(F32)).then_inc(filled, 16)

            def fill_row(stack, row, s, source, filled):
                sp.dma_start(stack[row:row + 1, s].bitcast(F32),
                             source.rearrange("a (o n) -> a o n", o=1).to_broadcast([1, HG, D])).then_inc(filled, 16)

            def fill_q(i, g):
                s = g % 2
                sp.wait_ge(qhi_ready, G * i + g + 1)
                if g == 0:
                    sp.wait_ge(x2_sum, C * (i + 1))
                if g == 0 or g == 1 and isinstance(i, int) and i == 0:
                    fill_row(qst, ROW_MASK, s, masks[B:B + 1, :], qst_in[s])
                fill(qst, s, ((0, q_hi), (2, q_hi)), qst_in[s])
                sp.wait_ge(q_split, G * i + g + 1)
                fill(qst, s, ((1, q_lo),), qst_in[s])

            def fill_k(i, g):
                s = g % 2
                if g < 2:
                    fill_row(kst, ROW_MASK, s, masks[bass.ds(i, 1), :], kst_in[s])
                if g == 0 or g == 1 and isinstance(i, int) and i == 0:
                    fill_row(kst, ROW_MAX, s, masks[B:B + 1, :], kst_in[s])
                sp.wait_ge(khi_ready, G * i + g + 1)
                fill(kst, s, ((0, k_hi), (1, k_hi)), kst_in[s])
                sp.wait_ge(k_split, G * i + g + 1)
                fill(kst, s, ((2, k_lo),), kst_in[s])

            def load_seq(i, kc):
                load(flat(seqT[bass.ds(i, 1), kc]), raw_seq(i, kc), w1_lo, C * i + kc + 1)

            def body(i, last):
                for kc in range(2, C):
                    load_seq(i, kc)
                fill_q(i, 0)
                fill_k(i, 0)
                if not last:
                    load_t(i + 1, sq_lo, C * i)
                for g in range(1, G):
                    fill_q(i, g)
                    fill_k(i, g)
                if not last:
                    load_x(i + 1, True, True)
                c = index(2, i, 0, 31)
                wait(sp, out_ready, C * i)
                sp.dma_start(bcol[:, B3], flat(b3[bass.ds(c, 1)])).then_inc(b3_in, 16)
                for m in range(C):
                    used, value = ((sq_lo, C * i + m + 1) if last
                                   else ((xb_lo, x1_lo)[m % 2], C * (i + 1) + 2 + m // 2 + 1))
                    load(flat(w3_blk[bass.ds(c, 1), m]), raw_w3(i, m, last), used, value)
                if not last:
                    load_w1(i + 1)
                for ready, stored in ((2, (1, 0)), (3, (2,)), (4, (3,))):
                    if ready == C and not last:
                        load_seq(i + 1, 0)
                        load_seq(i + 1, 1)
                    sp.wait_ge(out_ready, C * i + ready)
                    for m in stored:
                        sp.dma_start(flat(out[bass.ds(i, 1), m]), xres[:, m]).then_inc(out_kept[m], 16)

            for which, src in enumerate((steps, subjects, cats)):
                sp.dma_start(idx[0:1, which, :], src).then_inc(idx_in, 16)
            sp.wait_ge(idx_in, 3 * 16)
            load_t(0, None, 0)
            load_x(0, True, False)
            for dst, src in ((len_i[:, :], lengths), (xres[0:B, 0, :], iota), (cst[:, :], consts),
                             (bvec[:, 0, :], b_self), (bvec[:, 1, :], b_prev),
                             (bcol[:, BQ], bq), (bcol[:, BKSELF], bk), (bcol[:, BK], bk),
                             (bcol[:, BV], bv), (bcol[:, BO], bo)):
                sp.dma_start(dst, src).then_inc(consts_in, 16)
            load_x(0, False, True)
            for w, src in enumerate((wq, wk, wv, wo)):
                for n in range(C):
                    load(src[n], raw_shared(w, n), *((w_lo, 1 + C * (w - 1) + n + 1) if w
                                                     else ((xb_lo, x1_lo)[n % 2], 2 + n // 2 + 1)))
            sp.wait_ge(mask_made, 3)
            sp.dma_start(masks[0:B, :], xres[0:B, 1, :]).then_inc(mask_kept, 16)
            sp.dma_start(masks[B:B + 1, :], xres[0:1, 2, :]).then_inc(mask_kept, 16)
            load_w1(0)
            load_seq(0, 0)
            load_seq(0, 1)
            sp.wait_ge(mask_kept, 32)
            body(0, False)
            with sp.Fori(1, B - 1) as i:
                body(i, False)
            body(B - 1, True)
            for m in range(C):
                sp.wait_ge(out_kept[m], 16 * B)

        @block.tensor
        def _(pe):
            def product(dst, lhs, rhs, start, stop):
                pe.matmul(dst, lhs(0), rhs(0), start=start, stop=False)
                pe.matmul(dst, lhs(0), rhs(1), start=False, stop=False)
                return pe.matmul(dst, lhs(1), rhs(0), start=False, stop=stop)

            def chunk(m, kc, lhs, rhs, emptied, bank=None):
                if kc == 0:
                    wait(pe, *emptied)
                last = product(gb[m % 2][:, :] if bank is None else bank, lhs, rhs, kc == 0, kc == C - 1)
                if kc == C - 1:
                    last.then_inc(gemm_ready, 1)

            def l0(i, m, kc, before):
                if kc == 0:
                    pe.wait_ge(xb_lo, C * i + m + 1)
                if m == 0:
                    pe.wait_ge(t_lo, C * i + kc + 1)
                chunk(m, kc, lambda h: wblk[:, m % 2, h, cols(kc)], lambda h: ts_s[:, h, kc],
                      before[m] if m < 2 else (x1_sum, C * i + m - 1))

            def l1(i, m, kc):
                if kc == 0:
                    pe.wait_ge(w1_lo, C * i + m + 1)
                if m == 0:
                    pe.wait_ge(x1_lo, C * i + kc + 1)
                first = isinstance(i, int) and i == 0
                chunk(m, kc, lambda h: wblk[:, m % 2, h, cols(kc)], lambda h: (x1h, x1l)[h][:, kc],
                      (x2_part, C * i + m - 1) if m >= 2 else
                      (x1_sum, m + 3) if first else (out_ready, C * (i - 1) + m + 3))

            def projection(i, g, m, kc):
                if g == 0 and m == UNIT_Q:
                    pe.wait_ge(sq_lo, C * i + kc + 1)
                if g == 0 and m == UNIT_K:
                    pe.wait_ge(x2_lo, C * i + kc + 1)
                w = (wq_s, wk_s, wk_s, wv_s)[m]
                rhs = x2_s if m == UNIT_K else ts_s
                if m < 2:
                    emptied = ((x2_part, C * i + m + 3) if g == 0 else (v_ready, C * i + m + 3) if g == 1
                               else ((prod_ready, vself_ready)[m], G * i + g))
                else:
                    emptied = (qhi_ready, k_split)[m % 2], G * i + g + 1
                chunk(m, kc, lambda h: w[:, h, kc, cols(g)], lambda h: rhs[:, h, kc], emptied)

            def values(i, m, kc):
                chunk(m, kc, lambda h: x2_s[:, h, kc, cols(m)], lambda h: wv_s[:, h, kc],
                      (v_ready, C * i + m - 1) if m >= 2 else ((prod_ready, vself_ready)[m], G * i + 1))

            def l2_out(i, last, m, kc):
                if m == 0:
                    pe.wait_ge(at_lo, G * i + kc + 1)
                chunk(m, kc, lambda h: wo_s[:, h, kc, cols(m)], lambda h: at_s[:, h, kc],
                      (probs_ready, TILES * G * (i + 1)) if m >= 2 else
                      ((prod_ready, vself_ready)[m], G * i + G) if last else (x1_sum, C * (i + 1) + m + 3),
                      sc[m - 2][:, 0] if m >= 2 else None)

            def l3(i, m, kc):
                if kc == 0:
                    pe.wait_ge(w3_lo, C * i + m + 1)
                if m == 0:
                    pe.wait_ge(x3_lo, C * i + kc + 1)
                chunk(m, kc, lambda h: wblk[:, m % 2, h, cols(kc)], lambda h: x2_s[:, h, kc],
                      (out_ready, C * i + m - 1) if m >= 2 else (x3_sum, C * i + m + 1))

            def out_order(step):
                for m, kc in ([(m, kc) for m in range(C) for kc in range(C - 1) if m or kc]
                              + [(m, C - 1) for m in range(C)]):
                    step(m, kc)

            def l3_order(step):
                for m, kc in ([(0, 0), (1, 0), (0, 1), (1, 1), (0, 2), (0, 3), (1, 2), (1, 3)]
                              + [(m, kc) for m in range(2, C) for kc in range(C)]):
                    step(m, kc)

            def score_tile(t, lhs, rhs):
                for j in range(2):
                    mm = pe.matmul(sc[t % 2][:, j], lhs(j), rhs(j), start=True, stop=True)
                mm.then_inc(s_ready, 1)

            def body(i, last):
                for m in range(C):
                    for kc in range(C):
                        l1(i, m, kc)
                for m in range(C):
                    for kc in range(C):
                        projection(i, 0, m, kc)
                for m in range(C):
                    for kc in range(C):
                        values(i, m, kc)

                def max_tile(g, t):
                    slot, group, c, h0 = g % 2, G * i + g, t // 2, 2 * (t % 2)
                    if t == 0:
                        pe.wait_ge(qst_in[slot], q_filled(i, g))
                        pe.wait_ge(kst_in[slot], k_filled(i, g))
                    if t < 2:
                        wait(pe, probs_ready, TILES * group - 1 + t)
                        if g == 0:
                            wait(pe, x3_sum, C * i)
                    else:
                        pe.wait_ge(red_ready, TILES * group + t - 1)
                    score_tile(t, lambda j: qst[0:K_MAX, slot, h0 + j, cols(c)],
                               lambda j: kst[0:K_MAX, slot, h0 + j, :])

                for g in range(G):
                    slot, group = g % 2, G * i + g
                    before_l0 = ((prod_ready, G * i + G), (vself_ready, G * i + G))

                    def beside(n):
                        if g < G - 1:
                            projection(i, g + 1, n // C, n % C)
                        elif not last:
                            l0(i + 1, n // C, n % C, before_l0)

                    def self_scores():
                        pe.wait_ge(prod_ready, group + 1)
                        wait(pe, taken, group)
                        pe.matmul(dn[:, :], blocks, q_f[:, :], start=True, stop=True).then_inc(ss_ready, 1)

                    if g == 0:
                        for n in range(3):
                            beside(n)
                        self_scores()
                        max_tile(0, 0)
                    done = 3 if g == 0 else 0
                    for t, chunks in enumerate((0, 1, 1, 1, 1, 1, 1, 1) if g == 0 else (0, 1, 0, 1, 1, 1, 1, 3)):
                        if t:
                            max_tile(g, t)
                        for n in range(done, done + chunks):
                            beside(n)
                        done += chunks
                        if t == 2 and g:
                            self_scores()
                    pe.wait_ge(mxrep_ready, group + 1)
                    for c in range(C):
                        mm = pe.transpose(pv[:, cols(c)], mx_rep[:, cols(c)], ident)
                    mm.then_inc(mt_ready, 1)
                    for n in range(done, 14):
                        beside(n)

                    def prob_scores(t):
                        c, h0 = t // 2, 2 * (t % 2)
                        score_tile(t, lambda j: kst[0:K_ALL, slot, h0 + j, cols(c)],
                                   lambda j: qst[0:K_ALL, slot, h0 + j, :])

                    pe.wait_ge(negm_in, 16 * (group + 1))
                    pe.wait_ge(nself_ready, group + 1)
                    if g == 0:
                        pe.wait_ge(v_ready, C * i + C)
                    for t in range(2):
                        pe.wait_ge(red_ready, TILES * group + TILES - 1 + t)
                        prob_scores(t)
                    for n in range(14, 16):
                        beside(n)
                    for t in range(TILES):
                        c, h0 = t // 2, 2 * (t % 2)
                        if t == TILES - 1:
                            if g < G - 1:
                                max_tile(g + 1, 0)
                            else:
                                l2_out(i, last, 0, 0)
                        pe.wait_ge(probs_ready, TILES * group + t + 1)
                        for j in range(2):
                            row = DH * (h0 + j)
                            pe.matmul(pv[row:row + DH, :], v_sb[:, c, P * g + row:P * g + row + DH], probs[:, t % 2, j],
                                      start=(c == 0), stop=(c == C - 1), tile_position=(0, row))
                        for j in range(2):
                            row = (DH * (h0 + j) + P // 2) % P
                            mm = pe.matmul(dn[row:row + DH, :], ones, probs[:, t % 2, j], start=(c == 0),
                                           stop=(c == C - 1), tile_position=(0, row))
                        mm.then_inc(probs_used, 1)
                        if t + 2 < TILES:
                            prob_scores(t + 2)

                out_order(lambda m, kc: l2_out(i, last, m, kc))
                l3_order(lambda m, kc: l3(i, m, kc))

            for m in range(C):
                for kc in range(C):
                    l0(0, m, kc, ((x1_sum, 0), (x1_sum, 0)))
            for n, w in enumerate((wq_s, wk_s)):
                pe.wait_ge(w_lo, 1 + (n + 1) * C)
                for m in range(C):
                    for kc in range(C):
                        mm = product((pv, dn)[n][:, 2 * m:2 * m + 2], lambda h: w[:, h, kc, cols(m)],
                                     lambda h: bvs[:, h, kc], kc == 0, kc == C - 1)
                mm.then_inc(bias_mm, 1)
            pe.wait_ge(w_lo, 1 + 4 * C)
            pe.wait_ge(consts_in, 10 * 16)
            body(0, False)
            with pe.Fori(1, B - 1) as i:
                body(i, False)
            body(B - 1, True)

        @block.scalar
        def _(act):
            def hi(dst, slot_count, ready):
                slot, count = slot_count
                act.wait_ge(raw_in[slot], 16 * count)
                act.activation(dst, raw[:, slot], ACT.Copy).then_inc(ready, 1)

            def evacuate(dst, i, unit, bias, ready):
                act.wait_ge(gemm_ready, units(i) + unit + 1)
                act.activation(dst, gb[unit % 2][:, :], ACT.Identity, bias=bias).then_inc(ready, 1)

            def project_qk(i, g, first):
                evacuate(q_f[:, :], i, first + UNIT_Q, bcol[:, BQ, g:g + 1], q_ready)
                evacuate(q_hi[:, :], i, first + UNIT_Q, bcol[:, BQ, g:g + 1], qhi_ready)
                evacuate(k_hi[:, :], i, first + UNIT_K, bcol[:, BK, g:g + 1], khi_ready)

            def project_v(i, g, first):
                act.wait_ge(gemm_ready, units(i) + first + UNIT_VSELF + 1)
                wait(act, num_ready, G * i + g - 1)
                act.activation(vself[:, g % 2], gb[UNIT_VSELF % 2][:, :], ACT.Copy).then_inc(vself_ready, 1)

            def take_results(i, g):
                group = G * i + g
                act.wait_ge(probs_used, TILES * group + TILES)
                wait(act, at_lo, group)
                half = P // 2
                act.activation(den[0:half, :], dn[half:P, :], ACT.Copy)
                act.activation(den[half:P, :], dn[0:half, :], ACT.Copy)
                act.activation(num[:, :], pv[:, :], ACT.Copy).then_inc(taken, 1)

            def body(i, last):
                def w1_block(m):
                    act.wait_ge(gemm_ready, units(i) - 2 + m + 1)
                    hi(wblk[:, m % 2, 0], raw_w1(i, m), w1_hi)

                def seq_block(kc):
                    hi(ts_s[:, 0, kc], raw_seq(i, kc), sq_hi)

                w1_block(0)
                for m in range(1, C):
                    w1_block(m)
                    seq_block(m - 1)
                seq_block(C - 1)
                project_qk(i, 0, U_PROJ0)
                project_v(i, 0, U_PROJ0)
                for m in range(C):
                    act.wait_ge(gemm_ready, units(i) + U_V + m + 1)
                    act.activation(v_sb[:, m], gb[m % 2][:, :], ACT.Copy).then_inc(v_ready, 1)

                for g in range(G):
                    group, first = G * i + g, U_PROJ + C * g
                    if g:
                        take_results(i, g - 1)
                    if g == G - 1 and not last:
                        hi(wblk[:, 1, 0], raw_l0(i + 1, C + 2), xb_hi)
                    act.wait_ge(ss_ready, group + 1)
                    wait(act, den_ready, group)
                    act.activation(nself[:, :], dn[:, :], ACT.Copy, scale=-1.0).then_inc(nself_ready, 1)
                    if g < G - 1:
                        project_qk(i, g + 1, first)
                    elif not last:
                        for m in range(2, C):
                            act.wait_ge(gemm_ready, units(i) + U_L0 + m - 1)
                            hi(wblk[:, m % 2, 0], raw_l0(i + 1, C + 2 * m), xb_hi)
                    act.wait_ge(negm_ready, group + 1)
                    act.dma_start(qst[ROW_MAX:ROW_MAX + 1, g % 2].bitcast(F32), negm[0:P:DH, :].bitcast(F32)
                                  ).then_inc(negm_in, 16)
                    for t in range(TILES):
                        act.wait_ge(s_ready, 2 * TILES * group + TILES + t + 1)
                        wait(act, probs_used, TILES * group + t - 1)
                        act.activation(probs[:, t % 2], sc[t % 2][:, :, :], ACT.Exp, scale=SCALE
                                       ).then_inc(probs_ready, 1)
                        if t == 1 and g < G - 1:
                            project_v(i, g + 1, first)
                        if t == 2:
                            act.wait_ge(arg_ready, group + 1)
                            act.activation(nself[:, :], nself[:, :], ACT.Exp, scale=SCALE).then_inc(eself_ready, 1)
                        if g == G - 2 and 0 <= t - 3 < C and not last:
                            hi(ts_s[:, 0, t - 3], raw_l0(i + 1, t - 3), t_hi)
                    if g == G - 2 and not last:
                        hi(wblk[:, 0, 0], raw_l0(i + 1, C), xb_hi)
                take_results(i, G - 1)
                u_out = U_L0 + (0 if last else C)
                for m in range(2):
                    act.wait_ge(gemm_ready, units(i) + (U_L1 + m + 3 if last else U_L0 + m + 3))
                    hi(wblk[:, m % 2, 0], raw_w3(i, m, last), w3_hi)
                for m in range(C):
                    act.wait_ge(x3_sum, C * i + m + 1)
                    act.activation(x2_s[:, 0, m], xres[:, m], ACT.Copy).then_inc(x3_hi, 1)
                for m in range(2, C):
                    act.wait_ge(gemm_ready, units(i) + u_out + C + m - 1)
                    hi(wblk[:, m % 2, 0], raw_w3(i, m, last), w3_hi)

            for kc in range(C):
                hi(ts_s[:, 0, kc], raw_l0(0, kc), t_hi)
            for m in range(C):
                if m >= 2:
                    act.wait_ge(gemm_ready, m - 1)
                hi(wblk[:, m % 2, 0], raw_l0(0, C + 2 * m), xb_hi)
            act.wait_ge(consts_in, 10 * 16)
            act.activation(bvs[:, 0], bvec[:, :, :].rearrange("p v c -> p c v"), ACT.Copy).then_inc(w_hi, 1)
            for w, dst in enumerate((wq_s, wk_s, wv_s, wo_s)):
                for kc in range(C):
                    hi(dst[:, 0, kc], raw_shared(w, kc), w_hi)
            body(0, False)
            with act.Fori(1, B - 1) as i:
                body(i, False)
            body(B - 1, True)

        @block.gpsimd
        def _(pool):
            def lo(dst, hi_part, slot, hi_ready, count, ready):
                pool.wait_ge(hi_ready, count)
                pool.tensor_tensor(dst, raw[:, slot], hi_part.bitcast(F32), ALU.subtract).then_inc(ready, 1)

            def x_lo_block(i, m):
                lo(wblk[:, m % 2, 1], wblk[:, m % 2, 0], (2 * m) % C, xb_hi, C * i + m + 1, xb_lo)

            def split_q(i, g):
                pool.wait_ge(qhi_ready, G * i + g + 1)
                pool.tensor_tensor(q_lo[:, :], q_f[:, :], q_hi[:, :].bitcast(F32), ALU.subtract).then_inc(q_split, 1)

            def add_self(i, g):
                pool.wait_ge(taken, G * i + g + 1)
                if g < G - 1:
                    pool.tensor_tensor(den[:, :], den[:, :], nself[:, :], ALU.add).then_inc(den_ready, 1)
                pool.wait_ge(wself_ready, G * i + g + 1)
                pool.tensor_tensor(num[:, :], num[:, :], vself[:, g % 2], ALU.add).then_inc(num_ready, 1)

            def body(i, last):
                def w1_block(m):
                    lo(wblk[:, m % 2, 1], wblk[:, m % 2, 0], m, w1_hi, C * i + m + 1, w1_lo)

                def seq_block(kc):
                    lo(ts_s[:, 1, kc], ts_s[:, 0, kc], kc, sq_hi, C * i + kc + 1, sq_lo)

                w1_block(0)
                for m in range(1, C):
                    w1_block(m)
                    seq_block(m - 1)
                seq_block(C - 1)
                split_q(i, 0)
                for g in range(G):
                    group = G * i + g
                    if g:
                        add_self(i, g - 1)
                    if g < G - 1:
                        split_q(i, g + 1)
                    elif not last:
                        x_lo_block(i + 1, 1)
                        x_lo_block(i + 1, 2)
                        x_lo_block(i + 1, 3)
                    pool.wait_ge(negm_ready, group + 1)
                    pool.tensor_tensor(nself[:, :], negm[:, :].bitcast(F32), nself[:, :], ALU.subtract
                                       ).then_inc(arg_ready, 1)
                    pool.wait_ge(eself_ready, group + 1)
                    pool.tensor_tensor(vself[:, g % 2], vself[:, g % 2], nself[:, :], ALU.mult
                                       ).then_inc(wself_ready, 1)
                    if g == G - 2 and not last:
                        x_lo_block(i + 1, 0)
                add_self(i, G - 1)
                for m in range(C):
                    lo(wblk[:, m % 2, 1], wblk[:, m % 2, 0], m, w3_hi, C * i + m + 1, w3_lo)

            for m in range(C):
                x_lo_block(0, m)
            body(0, False)
            with pool.Fori(1, B - 1) as i:
                body(i, False)
            body(B - 1, True)

        @block.vector
        def _(dve):
            def lo(dst, hi_part, slot, hi_ready, count, ready):
                dve.wait_ge(hi_ready, count)
                dve.tensor_tensor(dst, raw[:, slot], hi_part.bitcast(F32), ALU.subtract).then_inc(ready, 1)

            def split(src, hi_part, lo_part, summed, hi_ready, lo_ready, count):
                dve.wait_ge(summed, count)
                dve.tensor_copy(hi_part, src).then_inc(hi_ready, 1)
                dve.wait_ge(hi_ready, count)
                dve.tensor_tensor(lo_part, src, hi_part.bitcast(F32), ALU.subtract).then_inc(lo_ready, 1)

            def t_lo_block(i, kc):
                lo(ts_s[:, 1, kc], ts_s[:, 0, kc], kc, t_hi, C * i + kc + 1, t_lo)

            def sum_x1(i, m, unit):
                slot, count = raw_l0(i, C + 2 * m + 1)
                dve.wait_ge(raw_in[slot], 16 * count)
                dve.wait_ge(gemm_ready, unit + m + 1)
                dve.tensor_tensor(raw[:, slot], gb[m % 2][:, :], raw[:, slot], ALU.add).then_inc(x1_sum, 1)

            def split_x1(i, m):
                slot, _ = raw_l0(i, C + 2 * m + 1)
                split(raw[:, slot], x1h[:, m], x1l[:, m], x1_sum, x1_hi, x1_lo, C * i + m + 1)

            def sum_x2(i, m):
                wait(dve, out_kept[m], 16 * i)
                dve.wait_ge(gemm_ready, units(i) + U_L1 + m + 1)
                dve.scalar_tensor_tensor(out=xres[:, m], in0=gb[m % 2][:, :], scalar=bcol[:, B1, m:m + 1],
                                         in1=x1h[:, m].bitcast(F32), op0=ALU.add, op1=ALU.add).then_inc(x2_part, 1)
                dve.wait_ge(x2_part, C * i + m + 1)
                dve.tensor_tensor(xres[:, m], xres[:, m], x1l[:, m].bitcast(F32), ALU.add).then_inc(x2_sum, 1)
                split(xres[:, m], x2_s[:, 0, m], x2_s[:, 1, m], x2_sum, x2_hi, x2_lo, C * i + m + 1)

            def add_to_xres(unit, m, bias, ready, bank=None):
                dve.wait_ge(gemm_ready, unit + m + 1)
                dve.scalar_tensor_tensor(out=xres[:, m], in0=gb[m % 2][:, :] if bank is None else bank, scalar=bcol[:, bias, m:m + 1],
                                         in1=xres[:, m], op0=ALU.add, op1=ALU.add).then_inc(ready, 1)

            def self_product(i, g, first):
                dve.wait_ge(gemm_ready, units(i) + first + UNIT_KSELF + 1)
                dve.wait_ge(q_split, G * i + g + 1)
                dve.scalar_tensor_tensor(out=q_f[:, :], in0=gb[UNIT_KSELF % 2][:, :], scalar=bcol[:, BKSELF, g:g + 1],
                                         in1=q_f[:, :], op0=ALU.add, op1=ALU.mult).then_inc(prod_ready, 1)

            def split_k(i, g):
                dve.wait_ge(khi_ready, G * i + g + 1)
                dve.scalar_tensor_tensor(out=k_lo[:, :], in0=gb[UNIT_K % 2][:, :], scalar=bcol[:, BK, g:g + 1],
                                         in1=k_hi[:, :].bitcast(F32), op0=ALU.add, op1=ALU.subtract
                                         ).then_inc(k_split, 1)

            def normalise(i, g):
                group = G * i + g
                dve.wait_ge(den_ready, group + 1)
                dve.reciprocal(den[:, :], den[:, :]).then_inc(recip_ready, 1)
                dve.wait_ge(num_ready, group + 1)
                dve.wait_ge(recip_ready, group + 1)
                dve.tensor_tensor(num[:, :], num[:, :], den[:, :], ALU.mult).then_inc(norm_ready, 1)
                dve.wait_ge(norm_ready, group + 1)
                dve.tensor_scalar(at_s[:, 0, g], num[:, :], bcol[:, BV, g:g + 1], None, ALU.add).then_inc(at_hi, 1)
                dve.wait_ge(at_hi, group + 1)
                dve.scalar_tensor_tensor(out=at_s[:, 1, g], in0=num[:, :], scalar=bcol[:, BV, g:g + 1],
                                         in1=at_s[:, 0, g].bitcast(F32), op0=ALU.add, op1=ALU.subtract
                                         ).then_inc(at_lo, 1)

            def body(i, last):
                dve.wait_ge(b1_in, 16 * (i + 1))
                for m in range(C):
                    sum_x2(i, m)
                split_k(i, 0)
                self_product(i, 0, U_PROJ0)
                l0_unit = units(i) + U_L0
                for g in range(G):
                    group, first = G * i + g, U_PROJ + C * g
                    wait(dve, mxrep_ready, group)
                    for t in range(TILES):
                        c, h0 = t // 2, 2 * (t % 2)
                        dve.wait_ge(s_ready, 2 * TILES * group + t + 1)
                        dve.tensor_reduce(mx[:, c, h0:h0 + 2], sc[t % 2][:, :, :], AX.X, ALU.max).then_inc(red_ready, 1)
                    dve.wait_ge(red_ready, TILES * (group + 1))
                    dve.tensor_copy(mx_rep.rearrange("p (a d) -> p a d", d=DH),
                                    mx[:, :, :].rearrange("p c (h o) -> p (c h) o", o=1)
                                    .to_broadcast([P, C * HG, DH])).then_inc(mxrep_ready, 1)
                    if g == G - 1 and not last:
                        sum_x1(i + 1, 0, l0_unit)
                    dve.wait_ge(mt_ready, group + 1)
                    dve.wait_ge(nself_ready, group + 1)
                    dve.scalar_tensor_tensor(out=negm[:, :], in0=pv[:, :], scalar=-1.0, in1=nself[:, :],
                                             op0=ALU.mult, op1=ALU.min).then_inc(negm_ready, 1)
                    if g < G - 1:
                        split_k(i, g + 1)
                        self_product(i, g + 1, first)
                    elif not last:
                        sum_x1(i + 1, 1, l0_unit)
                        split_x1(i + 1, 0)
                        split_x1(i + 1, 1)
                    if g:
                        normalise(i, g - 1)
                    if g == G - 2 and not last:
                        for kc in range(C):
                            t_lo_block(i + 1, kc)
                    if g == G - 1 and not last:
                        for m in range(2, C):
                            sum_x1(i + 1, m, l0_unit)
                            split_x1(i + 1, m)
                dve.wait_ge(taken, G * i + G)
                dve.tensor_tensor(den[:, :], den[:, :], nself[:, :], ALU.add).then_inc(den_ready, 1)
                normalise(i, G - 1)
                u_o = units(i) + U_L0 + (0 if last else C)
                for m in range(C + 1):
                    if m < C:
                        add_to_xres(u_o, m, BO, x3_sum, sc[m - 2][:, 0] if m >= 2 else None)
                    if m:
                        dve.wait_ge(x3_hi, C * i + m)
                        dve.tensor_tensor(x2_s[:, 1, m - 1], xres[:, m - 1], x2_s[:, 0, m - 1].bitcast(F32),
                                          ALU.subtract).then_inc(x3_lo, 1)
                dve.wait_ge(b3_in, 16 * (i + 1))
                for m in range(C):
                    add_to_xres(u_o + C, m, B3, out_ready)

            for kc in range(C):
                t_lo_block(0, kc)
            for m in range(C):
                sum_x1(0, m, 0)
                split_x1(0, m)
            dve.wait_ge(consts_in, 10 * 16)
            dve.tensor_copy(len_f[:, :], len_i[:, :]).then_inc(mask_made, 1)
            dve.memset(xres[0:1, 2, :], 1.0).then_inc(mask_made, 1)
            dve.wait_ge(mask_made, 2)
            dve.tensor_scalar(xres[0:B, 1, :], xres[0:B, 0, :], len_f[:, 0:1], MASKED, ALU.is_ge, ALU.mult
                              ).then_inc(mask_made, 1)
            dve.wait_ge(w_hi, 1)
            dve.tensor_tensor(bvs[:, 1], bvec[:, :, :].rearrange("p v c -> p c v"), bvs[:, 0].bitcast(F32),
                              ALU.subtract).then_inc(w_lo, 1)
            for w, dst in enumerate((wq_s, wk_s, wv_s, wo_s)):
                for kc in range(C):
                    lo(dst[:, 1, kc], dst[:, 0, kc], kc, w_hi, 1 + C * w + kc + 1, w_lo)
            for n, which, vec in ((0, BQ, 0), (1, BKSELF, 0), (1, BK, 1)):
                dve.wait_ge(bias_mm, n + 1)
                dve.tensor_tensor(bcol[:, which], (pv, dn)[n][:, 0:2 * C].rearrange("p (c v) -> p v c", v=2)[:, vec],
                                  bcol[:, which], ALU.add).then_inc(bias_ready, 1)
            dve.wait_ge(bias_ready, 3)
            dve.wait_ge(mask_kept, 32)
            body(0, False)
            with dve.Fori(1, B - 1) as i:
                body(i, False)
            body(B - 1, True)


def kernel(**inputs):
    import numpy as np
    import concourse.bacc as bacc
    from concourse.bass_utils import run_bass_kernel_spmd

    def arr(name):
        return np.asarray(inputs[name])

    def stationary(w):
        n = w.shape[0]
        return w.reshape(n, C, P, C, P).transpose(0, 3, 2, 1, 4).reshape(n, C, P, D)

    def transposed(w):
        return w.transpose(0, 2, 1).reshape(w.shape[0], C, P, D)

    def column(b):
        return b.reshape(-1, C, P).transpose(0, 2, 1)

    x, weight = arr("x"), arr("L1_cond_weight")
    consts = np.concatenate([np.eye(P), np.kron(np.eye(HG), np.ones((DH, DH))), np.ones((P, DH))], 1)
    data = {
        "x_blk": stationary(x), "xT": transposed(x), "Tt": transposed(arr("L0_cond_T")),
        "w1_blk": stationary(weight.transpose(0, 2, 1)), "b1": column(arr("L1_cond_bias")),
        "seqT": transposed(arr("fside_BxSxS_0")),
        "wq": arr("L2_cond_Wq").reshape(C, P, D), "wk": arr("L2_cond_Wk").reshape(C, P, D),
        "wv": arr("L2_cond_Wv").reshape(C, P, D), "wo": arr("L2_cond_Wo").reshape(C, P, D),
        "bq": column(arr("L2_cond_bq"))[0], "bk": column(arr("L2_cond_bk"))[0],
        "bv": column(arr("L2_cond_bv"))[0], "bo": column(arr("L2_cond_bo"))[0],
        "b_prev": column(arr("L2_cond_b_prev"))[0], "b_self": column(arr("L2_cond_b_self"))[0],
        "w3_blk": stationary(arr("L3_cond_W")), "b3": column(arr("L3_cond_b")),
        "steps": arr("itok_B_1_98").reshape(1, B), "subjects": arr("itok_B_0_7").reshape(1, B),
        "lengths": arr("itok_B_18_1004").reshape(B, 1), "cats": arr("itok_B_0_30").reshape(1, B),
        "consts": consts.astype(np.float32),
        "iota": np.tile(np.arange(D, dtype=np.float32), (B, 1)),
    }
    nc = bacc.Bacc("TRN2", target_bir_lowering=False, num_devices=1)
    arrays, args = {}, []
    for name, a in data.items():
        a = np.ascontiguousarray(a)
        arrays[f"in_{name}"] = a
        args.append(nc.dram_tensor(f"in_{name}", a.shape, mybir.dt.from_np(a.dtype), kind="ExternalInput").ap())
    out = nc.dram_tensor("out_t", (B, C, P, D), F32, kind="ExternalOutput").ap()
    build(nc, *args, out)
    r = run_bass_kernel_spmd(nc, [arrays], core_ids=[0])
    return r.results[0]["out_t"].reshape(B, D, D).transpose(0, 2, 1)
```
